# Optimizing a Trainium2 kernel written in Bass

```python
import numpy as np
import jax
import jax.numpy as jnp

def _softmax(x, axis=-1):
    return jax.nn.softmax(x, axis=axis)

def _gelu(x):
    return jax.nn.gelu(x, approximate=True)

def _silu(x):
    return jax.nn.silu(x)

def _sigmoid(x):
    return jax.nn.sigmoid(x)

def _layernorm(x, axis=-1, eps=1e-05):
    m = jnp.mean(x, axis=axis, keepdims=True)
    v = jnp.var(x, axis=axis, keepdims=True)
    return (x - m) / jnp.sqrt(v + eps)

def _scatter_add(tgt, idx, src, axis=0):
    return tgt.at[idx].add(src)

def _segment_sum(src, seg, n):
    return jax.ops.segment_sum(src, seg, n)
kernel_name = 'mk_adaln_d1_jaxref_r8_4ab6e0'

def setup_inputs(seed: int=0):
    np.random.seed(seed)
    _w = jnp.asarray

    def _L0_attn_setup():
        import jax, jax.numpy as jnp
        import numpy as np
        D_MODEL = 128
        NUM_HEADS = 16
        D_K = D_MODEL // NUM_HEADS
        BATCH, SEQ = (2, 256)
        key = jax.random.key(seed)
        k = jax.random.split(key, 5)
        std = np.sqrt(2.0 / (D_MODEL + D_MODEL)).astype(np.float32)
        return {'x': jax.random.normal(k[0], (BATCH, SEQ, D_MODEL), dtype=jnp.float32), 'WQ': jax.random.normal(k[1], (D_MODEL, D_MODEL), dtype=jnp.float32) * std, 'WK': jax.random.normal(k[2], (D_MODEL, D_MODEL), dtype=jnp.float32) * std, 'WV': jax.random.normal(k[3], (D_MODEL, D_MODEL), dtype=jnp.float32) * std, 'WO': jax.random.normal(k[4], (D_MODEL, D_MODEL), dtype=jnp.float32) * std}
    _L0_attn_in = _L0_attn_setup()

    def _L0_ffn_setup():
        import jax, jax.numpy as jnp
        import numpy as np
        from jax import lax
        T, B, I, M, O = (32, 64, 128, 128, 128)

        def _xavier(key, shape):
            fan_out, fan_in = shape
            limit = float(np.sqrt(6.0 / (fan_in + fan_out)))
            return jax.random.uniform(key, shape, jnp.float32, -limit, limit)
        key = jax.random.key(seed)
        ks = jax.random.split(key, 9)
        x = jax.random.normal(ks[0], (T, B, I), jnp.float32)
        return {'x': x, 'wf': _xavier(ks[1], (M, I)), 'uf': _xavier(ks[2], (M, M)), 'bf': jnp.zeros((M,), jnp.float32), 'wi': _xavier(ks[3], (M, I)), 'ui': _xavier(ks[4], (M, M)), 'bi': jnp.zeros((M,), jnp.float32), 'wc': _xavier(ks[5], (M, I)), 'uc': _xavier(ks[6], (M, M)), 'bc': jnp.zeros((M,), jnp.float32), 'wo': _xavier(ks[7], (O, I)), 'uo': _xavier(ks[8], (O, M)), 'bo': jnp.zeros((O,), jnp.float32), 'in_c': jnp.zeros((M,), jnp.float32)}
    _L0_ffn_in = _L0_ffn_setup()
    _L0_c = _w((lambda *s: np.random.randn(*s).astype(np.float32) * 0.05)(4, 128))
    _L0_wmod = _w((lambda *s: np.random.randn(*s).astype(np.float32) * 0.05)(128, 6 * 128) * 128 ** (-0.5))
    _d = {'L0_attn_x': _L0_attn_in['x'], 'L0_attn_WQ': _L0_attn_in['WQ'], 'L0_attn_WK': _L0_attn_in['WK'], 'L0_attn_WV': _L0_attn_in['WV'], 'L0_attn_WO': _L0_attn_in['WO'], 'L0_ffn_wf': _L0_ffn_in['wf'], 'L0_ffn_uf': _L0_ffn_in['uf'], 'L0_ffn_bf': _L0_ffn_in['bf'], 'L0_ffn_wi': _L0_ffn_in['wi'], 'L0_ffn_ui': _L0_ffn_in['ui'], 'L0_ffn_bi': _L0_ffn_in['bi'], 'L0_ffn_wc': _L0_ffn_in['wc'], 'L0_ffn_uc': _L0_ffn_in['uc'], 'L0_ffn_bc': _L0_ffn_in['bc'], 'L0_ffn_wo': _L0_ffn_in['wo'], 'L0_ffn_uo': _L0_ffn_in['uo'], 'L0_ffn_bo': _L0_ffn_in['bo'], 'L0_ffn_in_c': _L0_ffn_in['in_c'], 'L0_c': _L0_c, 'L0_wmod': _L0_wmod}
    _x0 = _d['L0_attn_x']
    _d['L0_attn_x'] = jax.random.normal(jax.random.fold_in(jax.random.key(seed), 1), (4, 512, 128), dtype=_x0.dtype)
    del _x0
    return _d

def reference(L0_attn_x, L0_attn_WQ, L0_attn_WK, L0_attn_WV, L0_attn_WO, L0_ffn_wf, L0_ffn_uf, L0_ffn_bf, L0_ffn_wi, L0_ffn_ui, L0_ffn_bi, L0_ffn_wc, L0_ffn_uc, L0_ffn_bc, L0_ffn_wo, L0_ffn_uo, L0_ffn_bo, L0_ffn_in_c, L0_c, L0_wmod):

    def _L0_attn_ref(x, WQ, WK, WV, WO):
        import jax, jax.numpy as jnp
        import numpy as np
        D_MODEL = 128
        NUM_HEADS = 16
        D_K = D_MODEL // NUM_HEADS
        BATCH, SEQ = (2, 256)
        B, S, E = x.shape
        mask = jnp.where(jnp.triu(jnp.ones((S, S), dtype=bool), k=1), -jnp.inf, 0.0).astype(x.dtype)

        def heads(W):
            return (x @ W).reshape(B, S, NUM_HEADS, D_K).transpose(0, 2, 1, 3)
        Q, K, V = (heads(WQ), heads(WK), heads(WV))
        score = jnp.einsum('bhqd,bhkd->bhqk', Q, K) / jnp.sqrt(jnp.asarray(D_K, x.dtype))
        score = score + mask
        score = score - jnp.max(score, axis=-1, keepdims=True)
        score = jnp.exp(score)
        score = score / jnp.sum(score, axis=-1, keepdims=True)
        out = jnp.einsum('bhqk,bhkd->bhqd', score, V)
        out = out.transpose(0, 2, 1, 3).reshape(B, S, E)
        return out @ WO

    def _L0_ffn_ref(x, wf, uf, bf, wi, ui, bi, wc, uc, bc, wo, uo, bo, in_c):
        import jax, jax.numpy as jnp
        import numpy as np
        from jax import lax
        T, B, I, M, O = (32, 64, 128, 128, 128)

        def _xavier(key, shape):
            fan_out, fan_in = shape
            limit = float(np.sqrt(6.0 / (fan_in + fan_out)))
            return jax.random.uniform(key, shape, jnp.float32, -limit, limit)
        batch = x.shape[1]
        c0 = jnp.broadcast_to(in_c, (batch, in_c.shape[0]))

        def step(c, xt):
            ft = jax.nn.sigmoid(xt @ wf.T + c @ uf.T + bf)
            it = jax.nn.sigmoid(xt @ wi.T + c @ ui.T + bi)
            gt = jnp.tanh(xt @ wc.T + c @ uc.T + bc)
            c = ft * c + it * gt
            return (c, None)
        c_final, _ = lax.scan(step, c0, x)
        h = jnp.tanh(jnp.einsum('tbi,oi->tbo', x, wo) + c_final @ uo.T + bo)
        return h
    x = L0_attn_x
    mod = (_silu(L0_c) @ L0_wmod).reshape(L0_c.shape[0], 6, 1, -1)
    sa, ca, ga, sb, cb, gb = (mod[:, 0], mod[:, 1], mod[:, 2], mod[:, 3], mod[:, 4], mod[:, 5])
    ga = (2 * (ga >= 0) - 1) * jnp.maximum(jnp.abs(ga), 0.25)
    gb = (2 * (gb >= 0) - 1) * jnp.maximum(jnp.abs(gb), 0.25)
    h = _layernorm(x, axis=-1) * (1 + ca) + sa
    x = x + ga * _L0_attn_ref(h, L0_attn_WQ, L0_attn_WK, L0_attn_WV, L0_attn_WO)
    h = _layernorm(x, axis=-1) * (1 + cb) + sb
    x = x + gb * _L0_ffn_ref(h, L0_ffn_wf, L0_ffn_uf, L0_ffn_bf, L0_ffn_wi, L0_ffn_ui, L0_ffn_bi, L0_ffn_wc, L0_ffn_uc, L0_ffn_bc, L0_ffn_wo, L0_ffn_uo, L0_ffn_bo, L0_ffn_in_c)
    return x

_drawn_inputs = setup_inputs


def setup_inputs(seed=0):
    import zlib

    import numpy as np

    out = dict(_drawn_inputs(seed))
    spreads = {'L0_ffn_bf': (0.0, 2.0),
     'L0_ffn_bi': (0.0, 2.0),
     'L0_ffn_bc': (0.0, 0.792),
     'L0_ffn_bo': (0.0, 0.495),
     'L0_ffn_in_c': (0.0, 0.8)}
    factors = {'L0_ffn_wf': 3.248, 'L0_ffn_uf': 6.904, 'L0_ffn_ui': 4.824}
    for name, (base, spread) in spreads.items():
        noise = np.random.default_rng([zlib.crc32(name.encode()), seed]).standard_normal(out[name].shape)
        drawn = base * np.exp(spread * noise) if base else spread * noise
        out[name] = jnp.asarray(drawn.astype(out[name].dtype))
    for name, factor in factors.items():
        out[name] = (out[name] * factor).astype(out[name].dtype)
    return out
```

```python
from contextlib import ExitStack

import concourse.bass as bass
from concourse import mybir

F32 = mybir.dt.float32
BF16 = mybir.dt.bfloat16
ALU = mybir.AluOpType
ACT = mybir.ActivationFunctionType
AX_X = mybir.AxisListType.X

P = 128
B, S, D = 4, 512, 128
H = 16
DK = D // H
NT = S // P
HG = 4
GB = H // HG
G = B * GB
NBANK = 10
SCALE = float(DK) ** -0.5
EPS = 1e-5
MASKED = -3.0e38

Q_PART = (0, 0, 0, 1, 1, 2)
K_PART = (0, 1, 2, 0, 1, 0)
MAX_ROW = DK * len(Q_PART)
CW = 32

EXP_LAG, PV_LAG = 2, 3


def work_order():
    work = [(-5, 0, "rows", 0), (-5, 1, "mod", 0), (0, 5, "w_in", 0), (1, 2, "w_state", 0), (2, 3, "ga", 0)]
    for b in range(B):
        s = GB * b
        work += [(s - 4, 8, "ln1_stats", b), (s - 3, 1, "ln1_apply", b), (s - 3, 3, "lnT1", b)]
        work += [(s - 3, 5, "q", b), (s - 3, 7, "k", b), (s - 3, 8, "store_q", b), (s - 3, 9, "store_k", b)]
        work += [(s - 2, 0, "stack", b), (s - 1, 5, "v", b)]
        work += [(s + 7, 4, "attnT", b), (s + 7, 6, "wo", b), (s + 7, 7, "ln2_stats", b)]
        work += [(s + 8, 0, "ln2_apply", b), (s + 8, 1, "lnT2", b)]
        work += [(s + 8, 4, "gate_f", b), (s + 8, 6, "gate_i", b), (s + 8, 8, "gate_c", b)]
    for g in range(G):
        work += [(g + 1, 0, "max_parts", g), (g + 1, 3, "maxT", g), (g + 1, 5, "max_rows", g)]
        work += [(g + PV_LAG + 1, 1, "outT", g)]
    return sorted(work, key=lambda w: w[:2])


WORK = work_order()
SHARED = ("rows", "mod", "w_in", "w_state", "ga", "lnT1", "q", "k", "v", "maxT", "outT", "attnT", "wo", "lnT2",
          "gate_f", "gate_i", "gate_c")
SHARED_AT = {w[2:]: n for n, w in enumerate(w for w in WORK if w[2] in SHARED)}
NORMS = [(w[2][:3], w[3]) for w in WORK if w[2] in ("ln1_stats", "ln2_stats")]
STEPS = [(s, k) for s in range(WORK[0][0], WORK[-1][0] + 1) for k in range(NBANK)]


def work_at(s, k):
    return [w[2:] for w in WORK if w[:2] == (s, k)]


def exp_bank(k):
    pair, j = divmod(k, NBANK // 2)
    a, b = 2 * pair, 2 * pair + 1
    return ([(a, 0, 0, 512)], [(b, 0, 0, 512)], [(a, 1, 0, 384), (a, 3, 384, 128)],
            [(b, 1, 0, 384), (b, 3, 384, 128)], [(a, 2, 0, 256), (b, 2, 256, 256)])[j]


def max_bank(k):
    pair, j = divmod(k, NBANK // 2)
    a, b = 2 * pair, 2 * pair + 1
    return ([(a, 3, 0, 512)], [(b, 3, 0, 512)], [(a, 2, 0, 384), (a, 0, 384, 128)],
            [(b, 2, 0, 384), (b, 0, 384, 128)], [(a, 1, 0, 256), (b, 1, 256, 256)])[j]


def strip(h, j):
    return next((k, c0) for k in range(NBANK) for hh, jj, c0, _ in exp_bank(k) if (hh, jj) == (h, j))


def adaln_block(nc, x, WQ, WK, WV, WO, wf, uf, bf, wi, ui, bi, wc, uc, bc, wo, uo, bo, in_c, c, wmod, out):
    ctx = ExitStack()
    with ctx:
        def sb(name, shape, dt=F32):
            return ctx.enter_context(nc.sbuf_tensor(name, shape, dt))

        def sem(name):
            return ctx.enter_context(nc.semaphore(name))

        parts_dram = nc.dram_tensor("parts", [B, 2, 3, P, S], BF16, kind="Internal")

        x_sb = sb("x_sb", [P, B, NT, D])
        x2_sb = sb("x2_sb", [P, B, NT, D])
        w_qkv = sb("w_qkv", [P, 3, D])
        wo_sb = sb("wo_sb", [P, D])
        wo_gated = sb("wo_gated", [P, B, D])
        ffn_w = sb("ffn_w", [P, 8, D])
        ffn_wT = sb("ffn_wT", [P, 8, D])
        wmod_sb = sb("wmod_sb", [P, 6 * D])
        rows = sb("rows", [B + 5, D])
        cols = sb("cols", [P, B + 5])
        half_bias = sb("half_bias", [P, 2])
        silu_sb = sb("silu_sb", [P, 3, B])
        silu_wide = sb("silu_wide", [P, B, P])
        mod = sb("mod", [P, 6, B])
        gb_sb = sb("gb_sb", [P, 3, B])
        ga_sb = sb("ga_sb", [P, 3, B * D])
        ident = sb("ident", [P, P])
        ident_b = sb("ident_b", [P, P], BF16)
        mask2 = sb("mask2", [P, 2, P], BF16)
        m_half = sb("m_half", [P, NT])
        stats = sb("stats", [P, 2, NT, 6])
        meanvar = sb("meanvar", [P, 2, NT, 2])
        rstd = sb("rstd", [P, 2, 2, NT])
        z_sb = sb("z_sb", [P, 2, NT, D])
        hT = sb("hT", [P, S])
        h2T = sb("h2T", [P, B, S])
        rem = sb("rem", [P, 2, S])
        parts = sb("parts_sb", [P, 2, 3, S], BF16)
        Qst = sb("Qst", [P, 2, H, S], BF16)
        Kst = sb("Kst", [P, 2, H, S], BF16)
        Vst = sb("Vst", [P, 2, NT, H, CW])
        negm = sb("negm", [P, 2, HG, NT])
        mrest = sb("mrest", [P, HG * NT])
        mparts = sb("mparts", [P, 2, 3, HG * NT], BF16)
        mrow = sb("mrow", [3 * HG * NT, 2, P], BF16)
        Pr = sb("Pr", [P, 2, NBANK, 512])
        oT = sb("oT", [P, 2, S])
        recip = sb("recip", [P, NT * HG])
        attn = sb("attn", [P, NT, D])
        attnT = sb("attnT", [P, S])
        gates = sb("gates", [P, 3, S])
        fc = sb("fc", [P, S])
        ig = sb("ig", [P, S])
        state2 = sb("state2", [P, S])
        h_out, hg = Pr[:, 0, 0:B], Pr[:, 0, B:2 * B]
        y_sb = Pr[:, 1, 0:B].rearrange("p b (i d) -> p b i d", i=NT)

        def bank(name):
            return ctx.enter_context(nc.psum_tensor(name, [P, 512], F32))

        ps_max = [bank(f"ps_max{n}") for n in range(3)]
        ps_exp = [bank(f"ps_exp{n}") for n in range(2)]
        ps_out = bank("ps_out")
        ps_shared = [bank(f"ps_shared{n}") for n in range(2)]
        ps_h = [ps_max[0], ps_max[1], ps_max[2], ps_out]
        ps_y = [ps_exp[0], ps_exp[1], ps_shared[0], ps_shared[1]]

        x_in = [sem(f"x_in{b}") for b in range(B)]
        rows_in, wmod_in, w_in, ffnw_in, wo_in = (sem(n) for n in ("rows_in", "wmod_in", "w_in", "ffnw_in", "wo_in"))
        ident_made, consts_made, stacks_clear, v_ones = (sem(n) for n in ("ident_made", "consts_made", "stacks_clear", "v_ones"))
        shared_filled = sem("shared_filled")
        shared_drained = [sem("shared_drained0"), sem("shared_drained1")]
        max_filled, max_drained = sem("max_filled"), sem("max_drained")
        exp_filled, exp_drained = sem("exp_filled"), sem("exp_drained")
        masked = sem("masked")
        out_filled, out_drained = sem("out_filled"), sem("out_drained")
        max_split, mrow_stored = sem("max_split"), [sem("mrow_in0"), sem("mrow_in1")]
        parts_hi, parts_mid, parts_lo = sem("parts_hi"), sem("parts_mid"), sem("parts_lo")
        parts_out = [sem("parts_out_q"), sem("parts_out_k")]
        stack_in = [sem("stack_in0"), sem("stack_in1")]
        ln_stats, ln_rstd, ln_z = sem("ln_stats"), sem("ln_rstd"), sem("ln_z")
        silu_tanh, silu_ready, mod_ready = sem("silu_tanh"), sem("silu_ready"), sem("mod_ready")
        wo_ready, wide_ready = sem("wo_ready"), sem("wide_ready")
        state_ready = sem("state_ready")
        h_filled, h_ready, hg_ready, y_filled, y_ready, y_out = (sem(n) for n in ("h_filled", "h_ready", "hg_ready", "y_filled", "y_ready", "y_out"))
        dve_step, pool_step, act_step = sem("dve_step"), sem("pool_step"), sem("act_step")

        def wait_filled(eng, kind, n):
            eng.wait_ge(shared_filled, SHARED_AT[kind, n] + 1)

        def shared_bank(kind, n):
            return ps_shared[SHARED_AT[kind, n] % 2]

        def drained_by(kind, n):
            return shared_drained[SHARED_AT[kind, n] % 2]

        def wait_drained(eng, kind, n):
            eng.wait_ge(drained_by(kind, n), SHARED_AT[kind, n] // 2 + 1)

        def stacks_loaded(b):
            return 16 * (12 * (b // 2 + 1) + b // 2)

        block = ctx.enter_context(nc.Block())

        @block.sync
        def _(sp):
            sp.dma_start(x_sb[:, 0], x[0].rearrange("(i p) d -> p i d", p=P)).then_inc(x_in[0], 16)
            sp.dma_start(wmod_sb[:], wmod[:, :]).then_inc(wmod_in, 16)
            for n, w in enumerate((WQ, WK, WV)):
                sp.dma_start(w_qkv[:, n], w[:, :]).then_inc(w_in, 16)
            for b in range(1, B):
                sp.dma_start(x_sb[:, b], x[b].rearrange("(i p) d -> p i d", p=P)).then_inc(x_in[b], 16)
            for s, k in STEPS:
                for kind, n in work_at(s, k):
                    if kind in ("store_q", "store_k"):
                        op = "qk".index(kind[-1])
                        sp.wait_ge(parts_lo, 2 * n + op + 1)
                        sp.dma_start(parts_dram[n, op].rearrange("t p s -> p t s"), parts[:, op]).then_inc(parts_out[op], 16)
                    elif kind == "stack":
                        if n < 2:
                            sp.wait_ge(stacks_clear, n + 1)
                        else:
                            sp.wait_ge(exp_filled, NBANK * GB * (n - 1))
                            sp.dma_start(Qst[MAX_ROW:MAX_ROW + 3, n % 2], Qst[96:99, n % 2]).then_inc(stack_in[n % 2], 16)
                        for op, (stack, part) in enumerate(((Qst, Q_PART), (Kst, K_PART))):
                            sp.wait_ge(parts_out[op], 16 * (n + 1))
                            for t, p in enumerate(part):
                                sp.dma_start(stack[DK * t:DK * (t + 1), n % 2],
                                             parts_dram[n, op, p].rearrange("(h d) s -> d h s", d=DK)).then_inc(stack_in[n % 2], 16)
                        if n == 0:
                            for i, w in enumerate((wf, wi, wc, wo, uf, ui, uc, uo)):
                                sp.dma_start(ffn_w[:, i], w[:, :]).then_inc(ffnw_in, 16)
                            sp.dma_start(wo_sb[:], WO[:, :]).then_inc(wo_in, 16)
                    elif kind == "max_rows":
                        wait_drained(sp, "maxT", n)
                        if n >= 2:
                            sp.wait_ge(mrow_stored[n % 2], 16 * (n // 2))
                        b, h = n // GB, HG * (n % GB)
                        sp.dma_start(Qst[MAX_ROW:MAX_ROW + 3, b % 2, h:h + HG, :], mrow[:, n % 2]).then_inc(mrow_stored[n % 2], 16)
            for b in range(B):
                sp.wait_ge(y_ready, b + 1)
                sp.dma_start(out[b].rearrange("(i p) d -> p i d", p=P), y_sb[:, b]).then_inc(y_out, 16)
            sp.wait_ge(y_out, 16 * B)

        @block.gpsimd
        def _(pool):
            steps = [0]

            def link(ins):
                steps[0] += 1
                ins.then_inc(pool_step, 1)
                pool.wait_ge(pool_step, steps[0])

            link(nc.gpsimd.memset(ident[:], 0.0))
            nc.gpsimd.affine_select(out=ident[:], in_=ident[:], compare_op=ALU.not_equal, fill=1.0, base=0,
                                    pattern=[[-1, P]], channel_multiplier=1).then_inc(ident_made, 1)
            nc.gpsimd.memset(m_half[:], -0.5)
            link(nc.gpsimd.memset(mask2[:], 0.0))
            pool.wait_ge(ident_made, 1)
            nc.gpsimd.tensor_copy(ident_b[:], ident[:])
            nc.gpsimd.affine_select(out=mask2[:], in_=mask2[:], compare_op=ALU.is_ge, fill=MASKED, base=0,
                                    pattern=[[0, 2], [-1, P]], channel_multiplier=1).then_inc(consts_made, 1)
            nc.gpsimd.memset(Qst[:, 0].rearrange("p h s -> p (h s)").bitcast(F32), 0.0)
            nc.gpsimd.memset(Kst[:, 0], 1.0).then_inc(stacks_clear, 1)
            for s, k in STEPS:
                for kind, n in work_at(s, k):
                    if kind in ("ln1_stats", "ln2_stats"):
                        m = NORMS.index((kind[:3], n))
                        pool.wait_ge(ln_stats, m + 1)
                        link(nc.gpsimd.tensor_scalar(rstd[:, m % 2, 0], meanvar[:, m % 2, :, 1], EPS, None, ALU.add))
                        nc.gpsimd.tensor_tensor(out=rstd[:, m % 2, 1], in0=rstd[:, m % 2, 0], in1=m_half[:],
                                                op=ALU.pow).then_inc(ln_rstd, 1)
                    elif kind in ("q", "k"):
                        op = "qk".index(kind)
                        pool.wait_ge(parts_mid, 2 * n + op + 1)
                        nc.gpsimd.tensor_tensor(out=parts[:, op, 2], in0=rem[:, op], in1=parts[:, op, 1],
                                                op=ALU.subtract).then_inc(parts_lo, 1)
                        if (kind, n) == ("k", 0):
                            nc.gpsimd.memset(Vst[:], 0.0)
                            link(nc.gpsimd.memset(Qst[:, 1].rearrange("p h s -> p (h s)").bitcast(F32), 0.0))
                            nc.gpsimd.memset(Vst[:, :, :, :, DK:DK + 1], 1.0).then_inc(v_ones, 1)
                            nc.gpsimd.memset(Kst[:, 1], 1.0).then_inc(stacks_clear, 1)
                    elif kind == "max_parts":
                        pool.wait_ge(max_drained, NBANK * (n + 1))
                        if n >= 2:
                            wait_filled(pool, "maxT", n - 2)
                        if n:
                            pool.wait_ge(max_split, n)
                        m, mp = negm[:, n % 2].rearrange("p h i -> p (h i)"), mparts[:, n % 2]
                        link(nc.gpsimd.tensor_copy(mp[:, 0], m))
                        link(nc.gpsimd.tensor_tensor(out=mrest[:], in0=m, in1=mp[:, 0], op=ALU.subtract))
                        link(nc.gpsimd.tensor_copy(mp[:, 1], mrest[:]))
                        nc.gpsimd.tensor_tensor(out=mp[:, 2], in0=mrest[:], in1=mp[:, 1], op=ALU.subtract).then_inc(max_split, 1)
                g = s - EXP_LAG
                if k % 5 == 4 and 0 <= g < G:
                    pool.wait_ge(exp_drained, NBANK * g + k + 1)
                    first = Pr[:, g % 2, k - 4:k]
                    for blocks in (first[:, :, 0:P], first[:, 2:4, 384:512],
                                   Pr[:, g % 2, k].rearrange("p (h q) -> p h q", h=2)[:, :, 0:P]):
                        last = nc.gpsimd.affine_select(out=blocks, in_=blocks, compare_op=ALU.is_ge, fill=0.0, base=0,
                                                       pattern=[[0, blocks.shape[1]], [1, P]], channel_multiplier=-1)
                    last.then_inc(masked, 1)

        @block.scalar
        def _(act):
            for n, v in enumerate((bf, bi, bc, bo, in_c)):
                act.dma_start(rows[B + n:B + n + 1, :], v.rearrange("(a n) -> a n", a=1)).then_inc(rows_in, 16)
            act.dma_start(rows[0:B, :], c[:, :]).then_inc(rows_in, 16)
            for s, k in STEPS:
                for kind, n in work_at(s, k):
                    if kind not in SHARED or kind in ("mod", "ga", "outT", "wo"):
                        continue
                    src, done = shared_bank(kind, n), drained_by(kind, n)
                    wait_filled(act, kind, n)
                    if kind == "rows":
                        nc.scalar.activation(cols[:], src[:, 0:B + 5], ACT.Copy).then_inc(done, 1)
                        wait_drained(act, kind, n)
                        nc.scalar.activation(silu_sb[:, 0], cols[:, 0:B], ACT.Tanh, scale=0.5).then_inc(silu_tanh, 1)
                        nc.scalar.activation(half_bias[:], cols[:, B:B + 2], ACT.Copy, scale=0.5).then_inc(act_step, 1)
                    elif kind == "w_in":
                        nc.scalar.activation(ffn_wT[:, 0:4].rearrange("p n m -> p (n m)"), src[:], ACT.Copy).then_inc(done, 1)
                    elif kind == "w_state":
                        nc.scalar.activation(ffn_wT[:, 4:8].rearrange("p n m -> p (n m)"), src[:], ACT.Copy, scale=0.5).then_inc(done, 1)
                    elif kind == "lnT1":
                        act.wait_ge(mod_ready, 1)
                        if n:
                            wait_filled(act, "v", n - 1)
                        nc.scalar.activation(hT[:], src[:], ACT.Identity, scale=mod[:, 1, n:n + 1],
                                             bias=mod[:, 0, n:n + 1]).then_inc(done, 1)
                    elif kind in ("q", "k"):
                        op = "qk".index(kind)
                        if n:
                            act.wait_ge(parts_out[op], 16 * n)
                        nc.scalar.activation(parts[:, op, 0], src[:], ACT.Copy).then_inc(parts_hi, 1)
                    elif kind == "v":
                        act.wait_ge(v_ones, 1)
                        if n >= 2:
                            act.wait_ge(out_filled, GB * (n - 1))
                        nc.scalar.activation(Vst[:, n % 2, :, :, 0:DK], src[:].rearrange("p (i h d) -> p i h d", i=NT, d=DK),
                                             ACT.Copy).then_inc(done, 1)
                    elif kind == "maxT":
                        if n >= 2:
                            act.wait_ge(mrow_stored[n % 2], 16 * (n // 2))
                        nc.scalar.activation(mrow[:, n % 2], src[0:3 * HG * NT, 0:P // 2].bitcast(BF16), ACT.Copy).then_inc(done, 1)
                    elif kind == "attnT":
                        if n:
                            wait_filled(act, "wo", n - 1)
                        nc.scalar.activation(attnT[:], src[:], ACT.Copy).then_inc(done, 1)
                    elif kind == "lnT2":
                        nc.scalar.activation(h2T[:, n], src[:], ACT.Identity, scale=mod[:, 4, n:n + 1],
                                             bias=mod[:, 3, n:n + 1]).then_inc(done, 1)
                    else:
                        i = "fic".index(kind[-1])
                        if (kind, n) == ("gate_f", 0):
                            act.wait_ge(act_step, 1)
                        act.wait_ge(state_ready, n + 1)
                        nc.scalar.activation(gates[:, i], src[:], ACT.Tanh, scale=1.0 if kind == "gate_c" else 0.5,
                                             bias=cols[:, B + 2:B + 3] if kind == "gate_c" else half_bias[:, i:i + 1]).then_inc(done, 1)
                g = s - EXP_LAG
                if 0 <= g < G:
                    if k == 0 and g >= 2:
                        act.wait_ge(out_filled, g - 1)
                    act.wait_ge(exp_filled, NBANK * g + k + 1)
                    nc.scalar.activation(Pr[:, g % 2, k], ps_exp[(NBANK * g + k) % 2][:], ACT.Exp, scale=SCALE).then_inc(exp_drained, 1)
                g = s - PV_LAG
                if k == 8 and 0 <= g < G:
                    act.wait_ge(out_filled, g + 1)
                    if g >= 2:
                        wait_filled(act, "outT", g - 2)
                    nc.scalar.activation(oT[:, g % 2], ps_out[:], ACT.Copy).then_inc(out_drained, 1)
            for t in range(B):
                act.wait_ge(h_filled, t + 1)
                nc.scalar.activation(h_out[:, t], ps_h[t][:], ACT.Tanh, bias=cols[:, B + 3:B + 4]).then_inc(h_ready, 1)

        @block.vector
        def _(dve):
            steps = [0]

            def link(ins):
                steps[0] += 1
                ins.then_inc(dve_step, 1)
                dve.wait_ge(dve_step, steps[0])

            def signed_floor(out_, gate, sign, magnitude):
                link(nc.vector.tensor_scalar(sign, gate, 0.0, 2.0, ALU.is_ge, ALU.mult))
                link(nc.vector.scalar_tensor_tensor(out=magnitude, in0=gate, scalar=-1.0, in1=gate, op0=ALU.mult, op1=ALU.max))
                link(nc.vector.tensor_scalar(magnitude, magnitude, 0.25, None, ALU.max))
                link(nc.vector.scalar_tensor_tensor(out=out_, in0=sign, scalar=1.0, in1=magnitude, op0=ALU.subtract, op1=ALU.mult))

            for s, k in STEPS:
                for kind, n in work_at(s, k):
                    if kind in ("mod", "ga", "wo", "outT"):
                        wait_filled(dve, kind, n)
                        src, done = shared_bank(kind, n), drained_by(kind, n)
                    if kind == "rows":
                        dve.wait_ge(silu_tanh, 1)
                        link(nc.vector.scalar_tensor_tensor(out=silu_sb[:, 1], in0=silu_sb[:, 0], scalar=1.0, in1=cols[:, 0:B],
                                                            op0=ALU.add, op1=ALU.mult))
                        nc.vector.tensor_scalar(silu_sb[:, 2], silu_sb[:, 1], 0.5, None, ALU.mult).then_inc(silu_ready, 1)
                    elif kind == "mod":
                        nc.vector.tensor_copy(mod[:].rearrange("p m b -> p (m b)"), src[:, 0:6 * B]).then_inc(done, 1)
                        wait_drained(dve, kind, n)
                        for m in (1, 4):
                            last = nc.vector.tensor_scalar(mod[:, m], mod[:, m], 1.0, None, ALU.add)
                        last.then_inc(mod_ready, 1)
                        signed_floor(gb_sb[:, 2], mod[:, 5], gb_sb[:, 0], gb_sb[:, 1])
                        dve.wait_ge(silu_ready, 1)
                        for b in range(B):
                            last = nc.vector.tensor_copy(silu_wide[:, b], silu_sb[:, 2, b:b + 1].broadcast_to([P, P]))
                        last.then_inc(wide_ready, 1)
                        link(nc.vector.memset(state2[:], 0.0))
                        nc.vector.tensor_scalar(state2[:], state2[:], cols[:, B + 4:B + 5], 2.0, ALU.add, ALU.mult).then_inc(state_ready, 1)
                    elif kind == "ga":
                        nc.vector.tensor_copy(ga_sb[:, 0], src[:]).then_inc(done, 1)
                        wait_drained(dve, kind, n)
                        signed_floor(ga_sb[:, 0], ga_sb[:, 0], ga_sb[:, 1], ga_sb[:, 2])
                        dve.wait_ge(wo_in, 16)
                        for b in range(B):
                            last = nc.vector.tensor_tensor(out=wo_gated[:, b], in0=wo_sb[:], in1=ga_sb[:, 0, b * D:(b + 1) * D], op=ALU.mult)
                        last.then_inc(wo_ready, 1)
                    elif kind in ("ln1_stats", "ln2_stats"):
                        m = NORMS.index((kind[:3], n))
                        if kind == "ln1_stats":
                            dve.wait_ge(x_in[n], 16)
                            src = x_sb[:, n]
                        else:
                            wait_drained(dve, "wo", n)
                            src = x2_sb[:, n]
                        if m >= 2:
                            dve.wait_ge(ln_rstd, m - 1)
                        for i in range(NT):
                            last = nc.vector.bn_stats(stats[:, m % 2, i], src[:, i])
                        link(last)
                        for i in range(NT):
                            last = nc.vector.bn_aggr(meanvar[:, m % 2, i], stats[:, m % 2, i])
                        last.then_inc(ln_stats, 1)
                    elif kind in ("ln1_apply", "ln2_apply"):
                        m = NORMS.index((kind[:3], n))
                        src = x_sb[:, n] if kind == "ln1_apply" else x2_sb[:, n]
                        dve.wait_ge(ln_rstd, m + 1)
                        if m >= 2:
                            wait_filled(dve, "lnT" + NORMS[m - 2][0][-1], NORMS[m - 2][1])
                        for i in range(NT):
                            last = nc.vector.tensor_scalar(z_sb[:, m % 2, i], src[:, i], meanvar[:, m % 2, i, 0:1],
                                                           rstd[:, m % 2, 1, i:i + 1], ALU.subtract, ALU.mult)
                        last.then_inc(ln_z, 1)
                    elif kind in ("q", "k"):
                        op = "qk".index(kind)
                        dve.wait_ge(parts_hi, 2 * n + op + 1)
                        nc.vector.tensor_tensor(out=rem[:, op], in0=shared_bank(kind, n)[:], in1=parts[:, op, 0],
                                                op=ALU.subtract).then_inc(drained_by(kind, n), 1)
                        wait_drained(dve, kind, n)
                        nc.vector.tensor_copy(parts[:, op, 1], rem[:, op]).then_inc(parts_mid, 1)
                    elif kind == "outT":
                        t = src[:].rearrange("p (i c v) -> p i c v", i=NT, v=CW)
                        if n and n % GB == 0:
                            wait_filled(dve, "attnT", n // GB - 1)
                        if n:
                            wait_drained(dve, "outT", n - 1)
                        r = recip[:].rearrange("p (i c) -> p i c", i=NT)
                        link(nc.vector.reciprocal(r, t[:, :, :, DK]))
                        h = HG * DK * (n % GB)
                        nc.vector.tensor_tensor(out=attn[:, :, h:h + HG * DK].rearrange("p i (c v) -> p i c v", v=DK),
                                                in0=t[:, :, :, 0:DK], in1=r.unsqueeze(3).broadcast_to([P, NT, HG, DK]),
                                                op=ALU.mult).then_inc(done, 1)
                    elif kind == "wo":
                        nc.vector.tensor_tensor(out=x2_sb[:, n].rearrange("p i d -> p (i d)"), in0=src[:],
                                                in1=x_sb[:, n].rearrange("p i d -> p (i d)"), op=ALU.add).then_inc(done, 1)
                    elif kind == "gate_c":
                        dve.wait_ge(state_ready, n + 1)
                        for name in ("gate_f", "gate_i", "gate_c"):
                            wait_drained(dve, name, n)
                        nc.vector.scalar_tensor_tensor(out=fc[:], in0=gates[:, 0], scalar=1.0, in1=state2[:], op0=ALU.add, op1=ALU.mult)
                        link(nc.vector.scalar_tensor_tensor(out=ig[:], in0=gates[:, 1], scalar=1.0, in1=gates[:, 2], op0=ALU.add, op1=ALU.mult))
                        nc.vector.scalar_tensor_tensor(out=state2[:], in0=fc[:], scalar=0.5, in1=ig[:], op0=ALU.mult, op1=ALU.add).then_inc(state_ready, 1)
                if 0 <= s < G:
                    g = s
                    if k == 0 and g >= 2:
                        dve.wait_ge(max_split, g - 1)
                    dve.wait_ge(max_filled, NBANK * g + k + 1)
                    pb = ps_max[(NBANK * g + k) % 3]
                    m = negm[:, g % 2]
                    tiles = max_bank(k)
                    if tiles[0][3] == tiles[-1][3]:
                        h0, i = tiles[0][:2]
                        nc.vector.tensor_reduce(out=m[:, h0:h0 + len(tiles), i], in_=pb[:].rearrange("p (h k) -> p h k", h=len(tiles)),
                                                axis=AX_X, op=ALU.max, negate=True).then_inc(max_drained, 1)
                    else:
                        for h, i, c0, w in tiles:
                            last = nc.vector.tensor_reduce(out=m[:, h, i:i + 1], in_=pb[:, c0:c0 + w], axis=AX_X, op=ALU.max, negate=True)
                        last.then_inc(max_drained, 1)
            for t in range(B):
                dve.wait_ge(h_ready, t + 1)
                nc.vector.tensor_scalar(hg[:, t], h_out[:, t], gb_sb[:, 2, t:t + 1], None, ALU.mult).then_inc(hg_ready, 1)
                dve.wait_ge(y_filled, t + 1)
                nc.vector.tensor_tensor(out=y_sb[:, t].rearrange("p i d -> p (i d)"), in0=ps_y[t][:],
                                        in1=x2_sb[:, t].rearrange("p i d -> p (i d)"), op=ALU.add).then_inc(y_ready, 1)

        @block.tensor
        def _(pe):
            def fills(ins):
                ins.then_inc(shared_filled, 1)

            for s, k in STEPS:
                if 0 <= s < G:
                    g = s
                    b, h0 = g // GB, HG * (g % GB)
                    if k == 0:
                        pe.wait_ge(stack_in[b % 2], stacks_loaded(b))
                        pe.wait_ge(consts_made, 1)
                    n = NBANK * g + k
                    if n >= 3:
                        pe.wait_ge(max_drained, n - 2)
                    pb = ps_max[n % 3]
                    for t, (h, i, c0, w) in enumerate(max_bank(k)):
                        nc.tensor.matmul(pb[:, c0:c0 + w], Qst[:, b % 2, h0 + h, P * i:P * (i + 1)], Kst[:, b % 2, h0 + h, 0:w],
                                         start=t == 0, stop=False, skip_group_check=True)
                    if k % 5 < 2:
                        diag, rhs = pb[:, 384:512], mask2[:, 0]
                    elif k % 5 < 4:
                        diag, rhs = pb[:, 256:512], mask2[:].rearrange("p a k -> p (a k)")
                    else:
                        diag, rhs = pb[:].rearrange("p (a k) -> p a k", a=2)[:, :, P:2 * P], mask2[:]
                    nc.tensor.matmul(diag, ident_b[:], rhs, start=False, stop=True, skip_group_check=True).then_inc(max_filled, 1)
                for kind, n in work_at(s, k):
                    if kind not in SHARED:
                        continue
                    at = SHARED_AT[kind, n]
                    if at >= 2:
                        pe.wait_ge(shared_drained[at % 2], at // 2)
                    pb = shared_bank(kind, n)
                    if kind == "rows":
                        pe.wait_ge(ident_made, 1)
                        pe.wait_ge(rows_in, 16 * 6)
                        fills(nc.tensor.transpose(pb[:, 0:B + 5], rows[:, :], ident[0:B + 5, 0:B + 5]))
                    elif kind in ("w_in", "w_state"):
                        pe.wait_ge(ffnw_in, 16 * 8)
                        for i in range(4):
                            last = nc.tensor.transpose(pb[:, P * i:P * (i + 1)], ffn_w[:, 4 * (kind == "w_state") + i], ident[:])
                        fills(last)
                    elif kind == "mod":
                        pe.wait_ge(silu_ready, 1)
                        pe.wait_ge(wmod_in, 16)
                        for m in range(6):
                            last = nc.tensor.matmul(pb[:, m * B:(m + 1) * B], wmod_sb[:, m * D:(m + 1) * D], silu_sb[:, 2], start=True, stop=True)
                        fills(last)
                    elif kind == "ga":
                        pe.wait_ge(wide_ready, 1)
                        for b in range(B):
                            last = nc.tensor.matmul(pb[:, b * D:(b + 1) * D], silu_wide[:, b], wmod_sb[:, 2 * D:3 * D], start=True, stop=True)
                        fills(last)
                    elif kind in ("lnT1", "lnT2"):
                        m = NORMS.index(("ln" + kind[-1], n))
                        pe.wait_ge(ln_z, m + 1)
                        for i in range(NT):
                            last = nc.tensor.transpose(pb[:, P * i:P * (i + 1)], z_sb[:, m % 2, i], ident[:])
                        fills(last)
                    elif kind in ("q", "k"):
                        wait_drained(pe, "lnT1", n)
                        pe.wait_ge(w_in, 16 * 3)
                        fills(nc.tensor.matmul(pb[:], w_qkv[:, "qk".index(kind)], hT[:], start=True, stop=True))
                    elif kind == "v":
                        for i in range(NT):
                            last = nc.tensor.matmul(pb[:, P * i:P * (i + 1)], hT[:, P * i:P * (i + 1)], w_qkv[:, 2], start=True, stop=True)
                        fills(last)
                    elif kind == "maxT":
                        pe.wait_ge(max_split, n + 1)
                        fills(nc.tensor.transpose(pb[0:3 * HG * NT, 0:P // 2].bitcast(BF16),
                                                  mparts[:, n % 2].rearrange("p t m -> p (t m)"), ident_b[:]))
                    elif kind == "outT":
                        pe.wait_ge(out_drained, n + 1)
                        for i in range(NT):
                            last = nc.tensor.transpose(pb[:, P * i:P * (i + 1)], oT[:, n % 2, P * i:P * (i + 1)], ident[:])
                        fills(last)
                    elif kind == "attnT":
                        wait_drained(pe, "outT", GB * n + GB - 1)
                        for i in range(NT):
                            last = nc.tensor.transpose(pb[:, P * i:P * (i + 1)], attn[:, i], ident[:])
                        fills(last)
                    elif kind == "wo":
                        wait_drained(pe, "attnT", n)
                        pe.wait_ge(wo_ready, 1)
                        for i in range(NT):
                            last = nc.tensor.matmul(pb[:, P * i:P * (i + 1)], attnT[:, P * i:P * (i + 1)], wo_gated[:, n], start=True, stop=True)
                        fills(last)
                    else:
                        i = "fic".index(kind[-1])
                        wait_drained(pe, "lnT2", n)
                        pe.wait_ge(state_ready, n + 1)
                        if (kind, n) == ("gate_f", 0):
                            wait_drained(pe, "w_in", 0)
                            wait_drained(pe, "w_state", 0)
                        nc.tensor.matmul(pb[:], ffn_wT[:, i], h2T[:, n], start=True, stop=False)
                        fills(nc.tensor.matmul(pb[:], ffn_wT[:, 4 + i], state2[:], start=False, stop=True))
                g = s - EXP_LAG
                if 0 <= g < G:
                    b, h0 = g // GB, HG * (g % GB)
                    if k == 0:
                        pe.wait_ge(mrow_stored[g % 2], 16 * (g // 2 + 1))
                    n = NBANK * g + k
                    if n >= 2:
                        pe.wait_ge(exp_drained, n - 1)
                    for h, j, c0, w in exp_bank(k):
                        last = nc.tensor.matmul(ps_exp[n % 2][:, c0:c0 + w], Kst[:, b % 2, h0 + h, P * j:P * (j + 1)],
                                                Qst[:, b % 2, h0 + h, P * j:S], start=True, stop=True)
                    last.then_inc(exp_filled, 1)
                g = s - PV_LAG
                if k in (1, 3, 5, 7) and 0 <= g < G:
                    j = k // 2
                    b, h0 = g // GB, HG * (g % GB)
                    if j == 0:
                        pe.wait_ge(masked, 2 * (g + 1))
                        wait_drained(pe, "v", b)
                        if g:
                            pe.wait_ge(out_drained, g)
                    for h in range(HG):
                        bk, c0 = strip(h, j)
                        last = nc.tensor.matmul(ps_out[CW * h:CW * (h + 1), P * j:S], Vst[:, b % 2, j, h0 + h],
                                                Pr[:, g % 2, bk, c0:c0 + S - P * j], start=j == 0, stop=j == NT - 1)
                    if j == NT - 1:
                        last.then_inc(out_filled, 1)
            pe.wait_ge(max_drained, NBANK * G)
            pe.wait_ge(out_drained, G)
            for t in range(B):
                nc.tensor.matmul(ps_h[t][:], ffn_wT[:, 3], h2T[:, t], start=True, stop=False)
            pe.wait_ge(state_ready, B + 1)
            for t in range(B):
                nc.tensor.matmul(ps_h[t][:], ffn_wT[:, 7], state2[:], start=False, stop=True).then_inc(h_filled, 1)
            pe.wait_ge(exp_drained, NBANK * G)
            for t in range(B):
                pe.wait_ge(hg_ready, t + 1)
                if t == 2:
                    wait_drained(pe, "gate_i", B - 1)
                    wait_drained(pe, "gate_c", B - 1)
                for i in range(NT):
                    last = nc.tensor.transpose(ps_y[t][:, P * i:P * (i + 1)], hg[:, t, P * i:P * (i + 1)], ident[:])
                last.then_inc(y_filled, 1)


_INS = ["L0_attn_x", "L0_attn_WQ", "L0_attn_WK", "L0_attn_WV", "L0_attn_WO", "L0_ffn_wf", "L0_ffn_uf", "L0_ffn_bf",
        "L0_ffn_wi", "L0_ffn_ui", "L0_ffn_bi", "L0_ffn_wc", "L0_ffn_uc", "L0_ffn_bc", "L0_ffn_wo", "L0_ffn_uo",
        "L0_ffn_bo", "L0_ffn_in_c", "L0_c", "L0_wmod"]


def kernel(**inputs):
    import numpy as np
    import concourse.bacc as bacc
    from concourse.bass_utils import run_bass_kernel_spmd

    nc = bacc.Bacc("TRN2", target_bir_lowering=False, num_devices=1)
    arrays, args = {}, []
    for name in _INS:
        a = np.ascontiguousarray(inputs[name])
        arrays[f"in_{name}"] = a
        args.append(nc.dram_tensor(f"in_{name}", a.shape, mybir.dt.from_np(a.dtype), kind="ExternalInput").ap())
    out = nc.dram_tensor("out", (B, S, D), F32, kind="ExternalOutput").ap()
    adaln_block(nc, *args, out)
    r = run_bass_kernel_spmd(nc, [arrays], core_ids=[0])
    return r.results[0]["out"]
```

```python
from contextlib import ExitStack

import concourse.bass as bass
from concourse import mybir

F32 = mybir.dt.float32
BF16 = mybir.dt.bfloat16
ALU = mybir.AluOpType
ACT = mybir.ActivationFunctionType
AX_X = mybir.AxisListType.X

P = 128
B, S, D = 4, 512, 128
H = 16
DK = D // H
NT = S // P
HG = 4
GB = H // HG
G = B * GB
NBANK = 10
SCALE = float(DK) ** -0.5
EPS = 1e-5
MASKED = -3.0e38
TWO_ONES = 1.001937866210938

Q_PART = (0, 0, 0, 1, 1, 2)
K_PART = (0, 1, 2, 0, 1, 0)
MAX_ROW = DK * len(Q_PART)
CW = 32

EXP_LAG, PV_LAG = 18, 30


def work_order():
    work = [(-58, "crow", 0), (-49, "silu", 0), (-48, "mod", 0), (-28, "wide", 0), (-24, "ga", 0), (-23, "floor", 0)]
    work += [(1, "bias", 0), (3, "w_in", 0), (6, "w_state", 0)]
    for b in range(B):
        t = GB * NBANK * b
        e = t - (54, 74, 54, 54)[b]
        work += [(e + i, "stat1", NT * b + i) for i in range(NT)] + [(e + 11 + i, "apply1", NT * b + i) for i in range(NT)]
        work += [(e + 4, "aggr1", b), (e + 17, "lnT1", b), (e + 20, "q", b), (e + 21, "mid_q", b), (e + 23, "k", b)]
        work += [(e + 24, "mid_k", b), (e + 25 if b < 2 else t - 22, "stack", b), (t - (29, 49, 13, 13)[b], "v", b)]
        work += [(t + 75 + i, "stat2", NT * b + i) for i in range(NT)] + [(t + 83 + i, "apply2", NT * b + i) for i in range(NT)]
        work += [(t + 71, "attnT", b), (t + 74, "wo", b), (t + 79, "aggr2", b)]
        if b < B - 1:
            work += [(t + 88, "lnT2", b), (t + 92, "gate_f", b), (t + 94, "forget", b), (t + 97, "gate_i", b)]
            work += [(t + 103, "gate_c", b), (t + 105, "state", b)]
    for g in range(G):
        t = NBANK * g
        work += [(t + 10, "max_parts", g), (t + 13, "maxT", g)]
        work += [(t + PV_LAG + 8, "out_copy", g), (t + PV_LAG + 10, "outT", g)]
    return sorted(work, key=lambda w: w[0])


WORK = work_order()
STEPS = range(WORK[0][0], WORK[-1][0] + 1)
SHARED = ("crow", "mod", "bias", "w_in", "w_state", "ga", "lnT1", "q", "k", "v", "maxT", "outT", "attnT", "wo", "lnT2",
          "gate_f", "gate_i", "gate_c")
LAST_SHARED = [("lnT2", B - 1), ("last_h", B - 1), ("last_y", B - 1)]
SHARED_AT = {w: n for n, w in enumerate([w[1:] for w in WORK if w[1] in SHARED] + LAST_SHARED)}
NORMS = [(w[1][-1], w[2]) for w in WORK if w[1] in ("aggr1", "aggr2")]


def work_at(t):
    return [w[1:] for w in WORK if w[0] == t]


def attention_at(t, lag):
    g, k = divmod(t - lag, NBANK)
    return (g, k) if 0 <= g < G else None


def exp_bank(k):
    pair, j = divmod(k, NBANK // 2)
    a, b = 2 * pair, 2 * pair + 1
    return ([(a, 0, 0, 512)], [(b, 0, 0, 512)], [(a, 1, 0, 384), (a, 3, 384, 128)],
            [(b, 1, 0, 384), (b, 3, 384, 128)], [(a, 2, 0, 256), (b, 2, 256, 256)])[j]


def max_bank(k):
    pair, j = divmod(k, NBANK // 2)
    a, b = 2 * pair, 2 * pair + 1
    return ([(a, 3, 0, 512)], [(b, 3, 0, 512)], [(a, 2, 0, 384), (a, 0, 384, 128)],
            [(b, 2, 0, 384), (b, 0, 384, 128)], [(a, 1, 0, 256), (b, 1, 256, 256)])[j]


def strip(h, j):
    return next((k, c0) for k in range(NBANK) for hh, jj, c0, _ in exp_bank(k) if (hh, jj) == (h, j))


def adaln_block(nc, x, WQ, WK, WV, WO, wf, uf, bf, wi, ui, bi, wc, uc, bc, wo, uo, bo, in_c, c, wmod, out):
    ctx = ExitStack()
    with ctx:
        def sb(name, shape, dt=F32):
            return ctx.enter_context(nc.sbuf_tensor(name, shape, dt))

        def sem(name):
            return ctx.enter_context(nc.semaphore(name))

        parts_dram = nc.dram_tensor("parts", [B, 2, 3, DK, H, S], BF16, kind="Internal")

        x_sb = sb("x_sb", [P, B, NT, D])
        x2_sb = sb("x2_sb", [P, B, NT, D])
        w_qkv = sb("w_qkv", [P, 3, D])
        wo_sb = sb("wo_sb", [P, D])
        wo_gated = sb("wo_gated", [P, B, D])
        ffn_w = sb("ffn_w", [P, 8, D])
        ffn_wT = sb("ffn_wT", [P, 8, D])
        wmod_sb = sb("wmod_sb", [P, 6 * D])
        c_rows = sb("c_rows", [B, D])
        c_cols = sb("c_cols", [P, B])
        bias_rows = sb("bias_rows", [5, D])
        bias_cols = sb("bias_cols", [P, 5])
        half_bias = sb("half_bias", [P, 2])
        silu_sb = sb("silu_sb", [P, 3, B])
        silu_wide = sb("silu_wide", [P, B, P])
        mod = sb("mod", [P, 6, B])
        gb_sb = sb("gb_sb", [P, 3, B])
        ga_sb = sb("ga_sb", [P, 3, B * D])
        ident = sb("ident", [P, P])
        ident_b = sb("ident_b", [P, P], BF16)
        mask = sb("mask", [P, S], BF16)
        
        m_half = sb("m_half", [P, NT])
        two_ones = sb("two_ones", [P, 1])
        stats = sb("stats", [P, 2, NT, 6])
        meanvar = sb("meanvar", [P, 2, NT, 2])
        rstd = sb("rstd", [P, 2, 2, NT])
        z_sb = sb("z_sb", [P, 2, NT, D])
        hT = sb("hT", [P, S])
        h2T = sb("h2T", [P, B, S])
        rem = sb("rem", [P, 2, S])
        parts = sb("parts_sb", [P, 2, 3, S], BF16)
        Qst = sb("Qst", [P, 2, H, S], BF16)
        Kst = sb("Kst", [P, 2, H, S], BF16)
        Vst = sb("Vst", [P, 2, NT, H, CW])
        negm = sb("negm", [P, 2, HG, NT])
        mrest = sb("mrest", [P, HG * NT])
        mparts = sb("mparts", [P, 2, 3, HG * NT], BF16)
        mrow = sb("mrow", [3 * HG * NT, 2, P], BF16)
        Pr = sb("Pr", [P, 2, NBANK, 512])
        oT = sb("oT", [P, 2, S])
        recip = sb("recip", [P, NT * HG])
        attn = sb("attn", [P, NT, D])
        attnT = sb("attnT", [P, S])
        gates = sb("gates", [P, 3, S])
        state2 = sb("state2", [P, S])
        fc, ig = ga_sb[:, 1], ga_sb[:, 2]
        h_out, hg = Pr[:, 0, 0:B], Pr[:, 0, B:2 * B]
        y_sb = Pr[:, 1, 0:B].rearrange("p b (i d) -> p b i d", i=NT)

        def bank(name):
            return ctx.enter_context(nc.psum_tensor(name, [P, 512], F32))

        ps_max = [bank(f"ps_max{n}") for n in range(3)]
        ps_exp = [bank(f"ps_exp{n}") for n in range(2)]
        ps_out = bank("ps_out")
        ps_shared = [bank(f"ps_shared{n}") for n in range(2)]
        ps_gate = ps_max
        ps_h = [ps_exp[0], ps_exp[1], ps_out, ps_shared[SHARED_AT["last_h", B - 1] % 2]]
        ps_y = [*ps_max, ps_shared[SHARED_AT["last_y", B - 1] % 2]]

        x_in = [sem(f"x_in{b}") for b in range(B)]
        c_in, bias_in, wmod_in, w_in, ffnw_in, wo_in = (sem(n) for n in ("c_in", "bias_in", "wmod_in", "w_in", "ffnw_in", "wo_in"))
        ident_made, consts_made, qst_clear, kst_set, v_ones = (sem(n) for n in ("ident_made", "consts_made", "qst_clear", "kst_set", "v_ones"))
        shared_filled = sem("shared_filled")
        shared_drained = [sem("shared_drained0"), sem("shared_drained1")]
        max_filled, max_drained = sem("max_filled"), sem("max_drained")
        exp_filled, exp_drained = sem("exp_filled"), sem("exp_drained")
        masked = sem("masked")
        out_filled, out_drained = sem("out_filled"), sem("out_drained")
        max_split, mrow_stored = sem("max_split"), [sem("mrow_in0"), sem("mrow_in1")]
        parts_hi, parts_mid, parts_lo = sem("parts_hi"), sem("parts_mid"), sem("parts_lo")
        parts_out = [[sem(f"parts_out_{o}{p}") for p in range(3)] for o in "qk"]
        stack_in = [sem("stack_in0"), sem("stack_in1")]
        first_heads_in = sem("first_heads_in")
        ln_tile, ln_stats, ln_rstd, ln_z = (sem(n) for n in ("ln_tile", "ln_stats", "ln_rstd", "ln_z"))
        silu_tanh, silu_ready, mod_ready = sem("silu_tanh"), sem("silu_ready"), sem("mod_ready")
        wo_ready, wide_ready = sem("wo_ready"), sem("wide_ready")
        state_ready, forget_ready = sem("state_ready"), sem("forget_ready")
        gate_filled, gate_ready = sem("gate_filled"), sem("gate_ready")
        pair_made, small_made = sem("pair_made"), sem("small_made")
        h_filled, h_ready, hg_ready, y_filled, y_ready, y_out = (sem(n) for n in ("h_filled", "h_ready", "hg_ready", "y_filled", "y_ready", "y_out"))
        dve_step, pool_step, act_step = sem("dve_step"), sem("pool_step"), sem("act_step")

        def wait_filled(eng, kind, n):
            eng.wait_ge(shared_filled, SHARED_AT[kind, n] + 1)

        def shared_bank(kind, n):
            return ps_shared[SHARED_AT[kind, n] % 2]

        def drained_by(kind, n):
            return shared_drained[SHARED_AT[kind, n] % 2]

        def wait_drained(eng, kind, n):
            eng.wait_ge(drained_by(kind, n), SHARED_AT[kind, n] // 2 + 1)

        def stacks_loaded(b):
            return 16 * (6 * (b // 2 + 1) + b // 2)

        RUNS = [(0, 3), (3, 2), (5, 1)]

        def stacks_ready(eng, g):
            b = g // GB
            if g == 0:
                eng.wait_ge(first_heads_in, 16 * 6)
            else:
                eng.wait_ge(stack_in[b % 2], stacks_loaded(b))

        block = ctx.enter_context(nc.Block())

        @block.sync
        def _(sp):
            def store_part(b, part):
                for op in range(2):
                    sp.wait_ge((parts_hi, parts_mid, parts_lo)[part], 2 * b + op + 1)
                    sp.dma_start(parts_dram[b, op, part].rearrange("d h s -> h d s"), parts[:, op, part]).then_inc(parts_out[op][part], 16)

            def load_run(b, op, run, h0, h1, done):
                t, many = RUNS[run]
                rows, part = slice(DK * t, DK * (t + many)), run if op == 0 else many - 1
                sp.wait_ge(parts_out[op][part], 16 * (b + 1))
                if op == 0:
                    src = parts_dram[b, 0, run, :, h0:h1].rearrange("d h s -> d (h s)").unsqueeze(0).broadcast_to([many, DK, (h1 - h0) * S])
                else:
                    src = parts_dram[b, 1, 0:many, :, h0:h1].rearrange("t d h s -> (t d) (h s)")
                sp.dma_start((Qst, Kst)[op][rows, b % 2, h0:h1], src).then_inc(done, 16)

            def load_high_middle(b, h0, h1, done):
                for op, run in ((0, 0), (1, 2), (0, 1), (1, 1)):
                    load_run(b, op, run, h0, h1, done)

            def load_low(b, h0, h1, done):
                for op, run in ((0, 2), (1, 0)):
                    load_run(b, op, run, h0, h1, done)

            sp.dma_start(x_sb[:, 0], x[0].rearrange("(i p) d -> p i d", p=P)).then_inc(x_in[0], 16)
            for n, w in enumerate((WQ, WK, WV)):
                sp.dma_start(w_qkv[:, n], w[:, :]).then_inc(w_in, 16)
            sp.dma_start(x_sb[:, 1], x[1].rearrange("(i p) d -> p i d", p=P)).then_inc(x_in[1], 16)
            sp.dma_start(wo_sb[:], WO[:, :]).then_inc(wo_in, 16)
            for n, v in enumerate((bf, bi, bc, bo, in_c)):
                sp.dma_start(bias_rows[n:n + 1, :], v.rearrange("(a n) -> a n", a=1)).then_inc(bias_in, 16)
            for i, w in enumerate((wf, wi, wc, wo, uf, ui, uc, uo)):
                sp.dma_start(ffn_w[:, i], w[:, :]).then_inc(ffnw_in, 16)
            for t in STEPS:
                for kind, n in work_at(t):
                    if kind == "stack":
                        store_part(n, 0)
                        if n == 1:
                            for b in range(2, B):
                                sp.dma_start(x_sb[:, b], x[b].rearrange("(i p) d -> p i d", p=P)).then_inc(x_in[b], 16)
                        store_part(n, 1)
                        if n < 2:
                            sp.wait_ge(qst_clear, n + 1)
                            sp.wait_ge(kst_set, n + 1)
                        else:
                            sp.wait_ge(exp_filled, NBANK * GB * (n - 1))
                            sp.dma_start(Qst[MAX_ROW:MAX_ROW + 3, n % 2], Qst[96:99, n % 2]).then_inc(stack_in[n % 2], 16)
                        first, done = (HG, first_heads_in) if n == 0 else (H, stack_in[n % 2])
                        load_high_middle(n, 0, first, done)
                        store_part(n, 2)
                        load_low(n, 0, first, done)
                        if n == 0:
                            load_high_middle(n, first, H, stack_in[0])
                            load_low(n, first, H, stack_in[0])
                    elif kind == "maxT":
                        wait_drained(sp, "maxT", n)
                        if n >= 2:
                            sp.wait_ge(mrow_stored[n % 2], 16 * (n // 2))
                        b, h = n // GB, HG * (n % GB)
                        sp.dma_start(Qst[MAX_ROW:MAX_ROW + 3, b % 2, h:h + HG, :], mrow[:, n % 2]).then_inc(mrow_stored[n % 2], 16)
            for b in range(B):
                sp.wait_ge(y_ready, b + 1)
                sp.dma_start(out[b].rearrange("(i p) d -> p i d", p=P), y_sb[:, b]).then_inc(y_out, 16)
            sp.wait_ge(y_out, 16 * B)

        @block.gpsimd
        def _(pool):
            steps = [0]

            def link(ins):
                steps[0] += 1
                ins.then_inc(pool_step, 1)
                pool.wait_ge(pool_step, steps[0])

            nc.gpsimd.memset(two_ones[:], TWO_ONES).then_inc(pair_made, 1)
            link(nc.gpsimd.memset(ident[:], 0.0))
            nc.gpsimd.affine_select(out=ident[:], in_=ident[:], compare_op=ALU.not_equal, fill=1.0, base=0,
                                    pattern=[[-1, P]], channel_multiplier=1).then_inc(ident_made, 1)
            nc.gpsimd.memset(Qst[:, 0].rearrange("p h s -> p (h s)").bitcast(F32), 0.0).then_inc(qst_clear, 1)
            nc.gpsimd.memset(m_half[:], -0.5).then_inc(small_made, 1)
            pool.wait_ge(small_made, 1)
            for t in STEPS:
                for kind, n in work_at(t):
                    if kind in ("aggr1", "aggr2"):
                        m = NORMS.index((kind[-1], n))
                        pool.wait_ge(ln_stats, m + 1)
                        link(nc.gpsimd.tensor_scalar(rstd[:, m % 2, 0], meanvar[:, m % 2, :, 1], EPS, None, ALU.add))
                        nc.gpsimd.tensor_tensor(out=rstd[:, m % 2, 1], in0=rstd[:, m % 2, 0], in1=m_half[:],
                                                op=ALU.pow).then_inc(ln_rstd, 1)
                        if (kind, n) == ("aggr1", 0):
                            link(nc.gpsimd.memset(mask[:], 0.0))
                            nc.gpsimd.tensor_copy(ident_b[:], ident[:])
                            nc.gpsimd.affine_select(out=mask[:], in_=mask[:], compare_op=ALU.is_ge, fill=MASKED, base=S - P,
                                                    pattern=[[-1, S]], channel_multiplier=1).then_inc(consts_made, 1)
                            link(nc.gpsimd.memset(Vst[:], 0.0))
                            nc.gpsimd.memset(Vst[:, :, :, :, DK:DK + 1], 1.0).then_inc(v_ones, 1)
                            nc.gpsimd.memset(Qst[:, 1].rearrange("p h s -> p (h s)").bitcast(F32), 0.0).then_inc(qst_clear, 1)
                    elif kind in ("mid_q", "mid_k"):
                        op = "qk".index(kind[-1])
                        pool.wait_ge(parts_mid, 2 * n + op + 1)
                        nc.gpsimd.tensor_tensor(out=parts[:, op, 2], in0=rem[:, op], in1=parts[:, op, 1],
                                                op=ALU.subtract).then_inc(parts_lo, 1)
                    elif kind == "max_parts":
                        pool.wait_ge(max_drained, NBANK * (n + 1))
                        if n >= 2:
                            wait_filled(pool, "maxT", n - 2)
                        if n:
                            pool.wait_ge(max_split, n)
                        m, mp = negm[:, n % 2].rearrange("p h i -> p (h i)"), mparts[:, n % 2]
                        link(nc.gpsimd.tensor_copy(mp[:, 0], m))
                        link(nc.gpsimd.tensor_tensor(out=mrest[:], in0=m, in1=mp[:, 0], op=ALU.subtract))
                        link(nc.gpsimd.tensor_copy(mp[:, 1], mrest[:]))
                        nc.gpsimd.tensor_tensor(out=mp[:, 2], in0=mrest[:], in1=mp[:, 1], op=ALU.subtract).then_inc(max_split, 1)
                at = attention_at(t, EXP_LAG)
                if at and at[1] % 5 == 4:
                    g, k = at
                    pool.wait_ge(exp_drained, NBANK * g + k + 1)
                    first = Pr[:, g % 2, k - 4:k]
                    for blocks in (first[:, :, 0:P], first[:, 2:4, 384:512],
                                   Pr[:, g % 2, k].rearrange("p (h q) -> p h q", h=2)[:, :, 0:P]):
                        last = nc.gpsimd.affine_select(out=blocks, in_=blocks, compare_op=ALU.is_ge, fill=0.0, base=0,
                                                       pattern=[[0, blocks.shape[1]], [1, P]], channel_multiplier=-1)
                    last.then_inc(masked, 1)

        @block.scalar
        def _(act):
            def tanh_gate(out_, src, i):
                return nc.scalar.activation(out_, src, ACT.Tanh, scale=0.5 if i < 2 else 1.0,
                                            bias=half_bias[:, i:i + 1] if i < 2 else bias_cols[:, 2:3])

            act.dma_start(c_rows[:], c[:, :]).then_inc(c_in, 16)
            act.dma_start(wmod_sb[:], wmod[:, :]).then_inc(wmod_in, 16)
            nc.scalar.preload_act_table(ACT.Exp)

            def set_key_rows(b):
                act.wait_ge(pair_made, 1)
                nc.scalar.activation(Kst[:, b].rearrange("p h s -> p (h s)").bitcast(F32),
                                     two_ones[:, 0:1].broadcast_to([P, H * S // 2]), ACT.Copy).then_inc(kst_set, 1)

            for t in STEPS:
                for kind, n in work_at(t):
                    if kind == "out_copy":
                        act.wait_ge(out_filled, n + 1)
                        if n >= 2:
                            wait_filled(act, "outT", n - 2)
                        nc.scalar.activation(oT[:, n % 2], ps_out[:], ACT.Copy).then_inc(out_drained, 1)
                    if kind not in SHARED or kind in ("mod", "ga", "outT", "wo"):
                        continue
                    src, done = shared_bank(kind, n), drained_by(kind, n)
                    wait_filled(act, kind, n)
                    if kind == "crow":
                        nc.scalar.activation(c_cols[:], src[:, 0:B], ACT.Copy).then_inc(done, 1)
                        wait_drained(act, kind, n)
                        nc.scalar.activation(silu_sb[:, 0], c_cols[:], ACT.Tanh, scale=0.5).then_inc(silu_tanh, 1)
                        set_key_rows(0)
                    elif kind == "bias":
                        nc.scalar.activation(bias_cols[:], src[:, 0:5], ACT.Copy).then_inc(done, 1)
                        wait_drained(act, kind, n)
                        nc.scalar.activation(half_bias[:], bias_cols[:, 0:2], ACT.Copy, scale=0.5).then_inc(act_step, 1)
                    elif kind == "w_in":
                        nc.scalar.activation(ffn_wT[:, 0:4].rearrange("p n m -> p (n m)"), src[:], ACT.Copy).then_inc(done, 1)
                    elif kind == "w_state":
                        nc.scalar.activation(ffn_wT[:, 4:8].rearrange("p n m -> p (n m)"), src[:], ACT.Copy, scale=0.5).then_inc(done, 1)
                    elif kind == "lnT1":
                        act.wait_ge(mod_ready, 1)
                        if n:
                            wait_filled(act, "v", n - 1)
                        nc.scalar.activation(hT[:], src[:], ACT.Identity, scale=mod[:, 1, n:n + 1],
                                             bias=mod[:, 0, n:n + 1]).then_inc(done, 1)
                    elif kind in ("q", "k"):
                        op = "qk".index(kind)
                        if n:
                            act.wait_ge(parts_out[op][0], 16 * n)
                        nc.scalar.activation(parts[:, op, 0], src[:], ACT.Copy).then_inc(parts_hi, 1)
                        if (kind, n) == ("k", 0):
                            set_key_rows(1)
                    elif kind == "v":
                        act.wait_ge(v_ones, 1)
                        if n >= 2:
                            act.wait_ge(out_filled, GB * (n - 1))
                        nc.scalar.activation(Vst[:, n % 2, :, :, 0:DK], src[:].rearrange("p (i h d) -> p i h d", i=NT, d=DK),
                                             ACT.Copy).then_inc(done, 1)
                    elif kind == "maxT":
                        if n >= 2:
                            act.wait_ge(mrow_stored[n % 2], 16 * (n // 2))
                        nc.scalar.activation(mrow[:, n % 2], src[0:3 * HG * NT, 0:P // 2].bitcast(BF16), ACT.Copy).then_inc(done, 1)
                    elif kind == "attnT":
                        if n:
                            wait_filled(act, "wo", n - 1)
                        nc.scalar.activation(attnT[:], src[:], ACT.Copy).then_inc(done, 1)
                    elif kind == "lnT2":
                        nc.scalar.activation(h2T[:, n], src[:], ACT.Identity, scale=mod[:, 4, n:n + 1],
                                             bias=mod[:, 3, n:n + 1]).then_inc(done, 1)
                    else:
                        i = "fic".index(kind[-1])
                        if (kind, n) == ("gate_f", 0):
                            act.wait_ge(act_step, 1)
                        act.wait_ge(state_ready, n + 2)
                        tanh_gate(gates[:, i], src[:], i).then_inc(done, 1)
                at = attention_at(t, EXP_LAG)
                if at:
                    g, k = at
                    if k == 0 and g >= 2:
                        act.wait_ge(out_filled, g - 1)
                    act.wait_ge(exp_filled, NBANK * g + k + 1)
                    nc.scalar.activation(Pr[:, g % 2, k], ps_exp[(NBANK * g + k) % 2][:], ACT.Exp, scale=SCALE).then_inc(exp_drained, 1)
            n = B - 1
            wait_filled(act, "lnT2", n)
            nc.scalar.activation(h2T[:, n], shared_bank("lnT2", n)[:], ACT.Identity, scale=mod[:, 4, n:n + 1],
                                 bias=mod[:, 3, n:n + 1]).then_inc(drained_by("lnT2", n), 1)
            act.wait_ge(state_ready, B + 1)
            for i in range(3):
                act.wait_ge(gate_filled, i + 1)
                tanh_gate(gates[:, i], ps_gate[i][:], i).then_inc(gate_ready, 1)
            for t in range(B):
                act.wait_ge(h_filled, t + 1)
                nc.scalar.activation(h_out[:, t], ps_h[t][:], ACT.Tanh, bias=bias_cols[:, 3:4]).then_inc(h_ready, 1)

        @block.vector
        def _(dve):
            steps = [0]

            def link(ins):
                steps[0] += 1
                ins.then_inc(dve_step, 1)
                dve.wait_ge(dve_step, steps[0])

            def signed_floor(out_, gate, sign, magnitude):
                link(nc.vector.tensor_scalar(sign, gate, 0.0, 2.0, ALU.is_ge, ALU.mult))
                link(nc.vector.scalar_tensor_tensor(out=magnitude, in0=gate, scalar=-1.0, in1=gate, op0=ALU.mult, op1=ALU.max))
                link(nc.vector.tensor_scalar(magnitude, magnitude, 0.25, None, ALU.max))
                link(nc.vector.scalar_tensor_tensor(out=out_, in0=sign, scalar=1.0, in1=magnitude, op0=ALU.subtract, op1=ALU.mult))

            def times_forget():
                nc.vector.scalar_tensor_tensor(out=fc[:], in0=gates[:, 0], scalar=1.0, in1=state2[:],
                                               op0=ALU.add, op1=ALU.mult).then_inc(forget_ready, 1)

            def new_state(n):
                link(nc.vector.scalar_tensor_tensor(out=ig[:], in0=gates[:, 1], scalar=1.0, in1=gates[:, 2], op0=ALU.add, op1=ALU.mult))
                dve.wait_ge(forget_ready, n + 1)
                nc.vector.scalar_tensor_tensor(out=state2[:], in0=fc[:], scalar=0.5, in1=ig[:], op0=ALU.mult,
                                               op1=ALU.add).then_inc(state_ready, 1)

            for t in STEPS:
                for kind, n in work_at(t):
                    if kind in ("mod", "ga", "wo", "outT"):
                        wait_filled(dve, kind, n)
                        src, done = shared_bank(kind, n), drained_by(kind, n)
                    if kind == "silu":
                        dve.wait_ge(silu_tanh, 1)
                        link(nc.vector.scalar_tensor_tensor(out=silu_sb[:, 1], in0=silu_sb[:, 0], scalar=1.0, in1=c_cols[:],
                                                            op0=ALU.add, op1=ALU.mult))
                        nc.vector.tensor_scalar(silu_sb[:, 2], silu_sb[:, 1], 0.5, None, ALU.mult).then_inc(silu_ready, 1)
                    elif kind == "mod":
                        nc.vector.tensor_copy(mod[:].rearrange("p m b -> p (m b)"), src[:, 0:6 * B]).then_inc(done, 1)
                        wait_drained(dve, kind, n)
                        for m in (1, 4):
                            last = nc.vector.tensor_scalar(mod[:, m], mod[:, m], 1.0, None, ALU.add)
                        last.then_inc(mod_ready, 1)
                    elif kind == "wide":
                        dve.wait_ge(silu_ready, 1)
                        for b in range(B):
                            last = nc.vector.tensor_copy(silu_wide[:, b], silu_sb[:, 2, b:b + 1].broadcast_to([P, P]))
                        last.then_inc(wide_ready, 1)
                        signed_floor(gb_sb[:, 2], mod[:, 5], gb_sb[:, 0], gb_sb[:, 1])
                        nc.vector.memset(state2[:], 0.0).then_inc(state_ready, 1)
                    elif kind == "bias":
                        dve.wait_ge(state_ready, 1)
                        wait_drained(dve, kind, n)
                        nc.vector.tensor_scalar(state2[:], state2[:], bias_cols[:, 4:5], 2.0, ALU.add, ALU.mult).then_inc(state_ready, 1)
                    elif kind == "ga":
                        nc.vector.tensor_copy(ga_sb[:, 0], src[:]).then_inc(done, 1)
                    elif kind == "floor":
                        wait_drained(dve, "ga", n)
                        signed_floor(ga_sb[:, 0], ga_sb[:, 0], ga_sb[:, 1], ga_sb[:, 2])
                        dve.wait_ge(wo_in, 16)
                        for b in range(B):
                            last = nc.vector.tensor_tensor(out=wo_gated[:, b], in0=wo_sb[:], in1=ga_sb[:, 0, b * D:(b + 1) * D], op=ALU.mult)
                        last.then_inc(wo_ready, 1)
                    elif kind in ("stat1", "stat2"):
                        b, i = divmod(n, NT)
                        m = NORMS.index((kind[-1], b))
                        if i == 0 and kind == "stat1":
                            dve.wait_ge(x_in[b], 16)
                        if i == 0 and kind == "stat2":
                            wait_drained(dve, "wo", b)
                        if i == 0 and m >= 2:
                            dve.wait_ge(ln_rstd, m - 1)
                        src = x_sb if kind == "stat1" else x2_sb
                        nc.vector.bn_stats(stats[:, m % 2, i], src[:, b, i]).then_inc(ln_tile, 1)
                    elif kind in ("aggr1", "aggr2"):
                        m = NORMS.index((kind[-1], n))
                        dve.wait_ge(ln_tile, NT * (m + 1))
                        for i in range(NT):
                            last = nc.vector.bn_aggr(meanvar[:, m % 2, i], stats[:, m % 2, i])
                        last.then_inc(ln_stats, 1)
                    elif kind in ("apply1", "apply2"):
                        b, i = divmod(n, NT)
                        m = NORMS.index((kind[-1], b))
                        src = x_sb if kind == "apply1" else x2_sb
                        if i == 0:
                            dve.wait_ge(ln_rstd, m + 1)
                            if m >= 2:
                                wait_filled(dve, "lnT" + NORMS[m - 2][0], NORMS[m - 2][1])
                        nc.vector.tensor_scalar(z_sb[:, m % 2, i], src[:, b, i], meanvar[:, m % 2, i, 0:1],
                                                rstd[:, m % 2, 1, i:i + 1], ALU.subtract, ALU.mult).then_inc(ln_z, 1)
                    elif kind in ("q", "k"):
                        op = "qk".index(kind)
                        dve.wait_ge(parts_hi, 2 * n + op + 1)
                        if n:
                            dve.wait_ge(parts_lo, 2 * n)
                        nc.vector.tensor_tensor(out=rem[:, op], in0=shared_bank(kind, n)[:], in1=parts[:, op, 0],
                                                op=ALU.subtract).then_inc(drained_by(kind, n), 1)
                    elif kind in ("mid_q", "mid_k"):
                        op = "qk".index(kind[-1])
                        wait_drained(dve, kind[-1], n)
                        if n:
                            dve.wait_ge(parts_out[op][1], 16 * n)
                            dve.wait_ge(parts_out[op][2], 16 * n)
                        nc.vector.tensor_copy(parts[:, op, 1], rem[:, op]).then_inc(parts_mid, 1)
                    elif kind == "outT":
                        prod = src[:].rearrange("p (i c v) -> p i c v", i=NT, v=CW)
                        if n and n % GB == 0:
                            wait_filled(dve, "attnT", n // GB - 1)
                        if n:
                            wait_drained(dve, "outT", n - 1)
                        r = recip[:].rearrange("p (i c) -> p i c", i=NT)
                        link(nc.vector.reciprocal(r, prod[:, :, :, DK]))
                        h = HG * DK * (n % GB)
                        nc.vector.tensor_tensor(out=attn[:, :, h:h + HG * DK].rearrange("p i (c v) -> p i c v", v=DK),
                                                in0=prod[:, :, :, 0:DK], in1=r.unsqueeze(3).broadcast_to([P, NT, HG, DK]),
                                                op=ALU.mult).then_inc(done, 1)
                    elif kind == "wo":
                        nc.vector.tensor_tensor(out=x2_sb[:, n].rearrange("p i d -> p (i d)"), in0=src[:],
                                                in1=x_sb[:, n].rearrange("p i d -> p (i d)"), op=ALU.add).then_inc(done, 1)
                    elif kind == "forget":
                        dve.wait_ge(state_ready, n + 2)
                        wait_drained(dve, "gate_f", n)
                        times_forget()
                    elif kind == "state":
                        wait_drained(dve, "gate_i", n)
                        wait_drained(dve, "gate_c", n)
                        new_state(n)
                at = attention_at(t, 0)
                if at:
                    g, k = at
                    if k == 0 and g == 0:
                        dve.wait_ge(consts_made, 1)
                    if k == 0 and g >= 2:
                        dve.wait_ge(max_split, g - 1)
                    dve.wait_ge(max_filled, NBANK * g + k + 1)
                    pb = ps_max[(NBANK * g + k) % 3]
                    m = negm[:, g % 2]
                    for h, i, c0, w in max_bank(k):
                        last = nc.vector.tensor_tensor_reduce(
                            out=pb[:, c0:c0 + w], in0=pb[:, c0:c0 + w], in1=mask[:, S - w:S], scale=-1.0, scalar=-MASKED,
                            op0=ALU.add, op1=ALU.min, accum_out=m[:, h, i:i + 1])
                    last.then_inc(max_drained, 1)
            dve.wait_ge(state_ready, B + 1)
            dve.wait_ge(gate_ready, 1)
            times_forget()
            dve.wait_ge(gate_ready, 3)
            new_state(B - 1)
            for t in range(B + 1):
                if t < B:
                    dve.wait_ge(h_ready, t + 1)
                    nc.vector.tensor_scalar(hg[:, t], h_out[:, t], gb_sb[:, 2, t:t + 1], None, ALU.mult).then_inc(hg_ready, 1)
                if t:
                    dve.wait_ge(y_filled, t)
                    nc.vector.tensor_tensor(out=y_sb[:, t - 1].rearrange("p i d -> p (i d)"), in0=ps_y[t - 1][:],
                                            in1=x2_sb[:, t - 1].rearrange("p i d -> p (i d)"), op=ALU.add).then_inc(y_ready, 1)

        @block.tensor
        def _(pe):
            def fills(ins):
                ins.then_inc(shared_filled, 1)

            def take_shared(kind, n):
                at = SHARED_AT[kind, n]
                if at >= 2:
                    pe.wait_ge(shared_drained[at % 2], at // 2)
                return shared_bank(kind, n)

            def transpose_norm(which, n):
                m = NORMS.index((which, n))
                pb = take_shared("lnT" + which, n)
                for i in range(NT):
                    pe.wait_ge(ln_z, NT * m + i + 1)
                    last = nc.tensor.transpose(pb[:, P * i:P * (i + 1)], z_sb[:, m % 2, i], ident[:])
                fills(last)

            for t in STEPS:
                at = attention_at(t, 0)
                if at:
                    g, k = at
                    b, h0 = g // GB, HG * (g % GB)
                    if k == 0:
                        stacks_ready(pe, g)
                    n = NBANK * g + k
                    if n >= 3:
                        pe.wait_ge(max_drained, n - 2)
                    pb = ps_max[n % 3]
                    for h, i, c0, w in max_bank(k):
                        last = nc.tensor.matmul(pb[:, c0:c0 + w], Qst[:, b % 2, h0 + h, P * i:P * (i + 1)], Kst[:, b % 2, h0 + h, 0:w],
                                                start=True, stop=True)
                    last.then_inc(max_filled, 1)
                for kind, n in work_at(t):
                    if kind not in SHARED:
                        continue
                    if kind in ("lnT1", "lnT2"):
                        transpose_norm(kind[-1], n)
                        continue
                    pb = take_shared(kind, n)
                    if kind == "crow":
                        pe.wait_ge(ident_made, 1)
                        pe.wait_ge(c_in, 16)
                        fills(nc.tensor.transpose(pb[:, 0:B], c_rows[:, :], ident[0:B, 0:B]))
                    elif kind == "bias":
                        pe.wait_ge(bias_in, 16 * 5)
                        fills(nc.tensor.transpose(pb[:, 0:5], bias_rows[:, :], ident[0:5, 0:5]))
                    elif kind in ("w_in", "w_state"):
                        pe.wait_ge(ffnw_in, 16 * 8)
                        for i in range(4):
                            last = nc.tensor.transpose(pb[:, P * i:P * (i + 1)], ffn_w[:, 4 * (kind == "w_state") + i], ident[:])
                        fills(last)
                    elif kind == "mod":
                        pe.wait_ge(silu_ready, 1)
                        pe.wait_ge(wmod_in, 16)
                        for m in range(6):
                            last = nc.tensor.matmul(pb[:, m * B:(m + 1) * B], wmod_sb[:, m * D:(m + 1) * D], silu_sb[:, 2], start=True, stop=True)
                        fills(last)
                    elif kind == "ga":
                        pe.wait_ge(wide_ready, 1)
                        for b in range(B):
                            last = nc.tensor.matmul(pb[:, b * D:(b + 1) * D], silu_wide[:, b], wmod_sb[:, 2 * D:3 * D], start=True, stop=True)
                        fills(last)
                    elif kind in ("q", "k"):
                        wait_drained(pe, "lnT1", n)
                        pe.wait_ge(w_in, 16 * 3)
                        fills(nc.tensor.matmul(pb[:], w_qkv[:, "qk".index(kind)], hT[:], start=True, stop=True))
                    elif kind == "v":
                        for i in range(NT):
                            last = nc.tensor.matmul(pb[:, P * i:P * (i + 1)], hT[:, P * i:P * (i + 1)], w_qkv[:, 2], start=True, stop=True)
                        fills(last)
                    elif kind == "maxT":
                        pe.wait_ge(max_split, n + 1)
                        fills(nc.tensor.transpose(pb[0:3 * HG * NT, 0:P // 2].bitcast(BF16),
                                                  mparts[:, n % 2].rearrange("p t m -> p (t m)"), ident_b[:]))
                    elif kind == "outT":
                        pe.wait_ge(out_drained, n + 1)
                        for i in range(NT):
                            last = nc.tensor.transpose(pb[:, P * i:P * (i + 1)], oT[:, n % 2, P * i:P * (i + 1)], ident[:])
                        fills(last)
                    elif kind == "attnT":
                        wait_drained(pe, "outT", GB * n + GB - 1)
                        for i in range(NT):
                            last = nc.tensor.transpose(pb[:, P * i:P * (i + 1)], attn[:, i], ident[:])
                        fills(last)
                    elif kind == "wo":
                        wait_drained(pe, "attnT", n)
                        pe.wait_ge(wo_ready, 1)
                        for i in range(NT):
                            last = nc.tensor.matmul(pb[:, P * i:P * (i + 1)], attnT[:, P * i:P * (i + 1)], wo_gated[:, n], start=True, stop=True)
                        fills(last)
                    else:
                        i = "fic".index(kind[-1])
                        pe.wait_ge(state_ready, n + 2)
                        if (kind, n) == ("gate_f", 0):
                            wait_drained(pe, "w_in", 0)
                            wait_drained(pe, "w_state", 0)
                        nc.tensor.matmul(pb[:], ffn_wT[:, 4 + i], state2[:], start=True, stop=False)
                        wait_drained(pe, "lnT2", n)
                        fills(nc.tensor.matmul(pb[:], ffn_wT[:, i], h2T[:, n], start=False, stop=True))
                at = attention_at(t, EXP_LAG)
                if at:
                    g, k = at
                    b, h0 = g // GB, HG * (g % GB)
                    if k == 0:
                        pe.wait_ge(mrow_stored[g % 2], 16 * (g // 2 + 1))
                    n = NBANK * g + k
                    if n >= 2:
                        pe.wait_ge(exp_drained, n - 1)
                    for h, j, c0, w in exp_bank(k):
                        last = nc.tensor.matmul(ps_exp[n % 2][:, c0:c0 + w], Kst[:, b % 2, h0 + h, P * j:P * (j + 1)],
                                                Qst[:, b % 2, h0 + h, P * j:S], start=True, stop=True)
                    last.then_inc(exp_filled, 1)
                at = attention_at(t, PV_LAG)
                if at and at[1] in (0, 2, 4, 6):
                    g, j = at[0], at[1] // 2
                    b, h0 = g // GB, HG * (g % GB)
                    if j == 0:
                        pe.wait_ge(masked, 2 * (g + 1))
                        wait_drained(pe, "v", b)
                        if g:
                            pe.wait_ge(out_drained, g)
                    for h in range(HG):
                        bk, c0 = strip(h, j)
                        last = nc.tensor.matmul(ps_out[CW * h:CW * (h + 1), P * j:S], Vst[:, b % 2, j, h0 + h],
                                                Pr[:, g % 2, bk, c0:c0 + S - P * j], start=j == 0, stop=j == NT - 1)
                    if j == NT - 1:
                        last.then_inc(out_filled, 1)
            pe.wait_ge(max_drained, NBANK * G)
            pe.wait_ge(state_ready, B + 1)
            for i in range(3):
                nc.tensor.matmul(ps_gate[i][:], ffn_wT[:, 4 + i], state2[:], start=True, stop=False)
            pe.wait_ge(exp_drained, NBANK * G)
            pe.wait_ge(out_drained, G)
            for t in range(B - 1):
                nc.tensor.matmul(ps_h[t][:], ffn_wT[:, 3], h2T[:, t], start=True, stop=False)
            transpose_norm("2", B - 1)
            wait_drained(pe, "lnT2", B - 1)
            for i in range(3):
                nc.tensor.matmul(ps_gate[i][:], ffn_wT[:, i], h2T[:, B - 1], start=False, stop=True).then_inc(gate_filled, 1)
            take_shared("last_h", B - 1)
            nc.tensor.matmul(ps_h[B - 1][:], ffn_wT[:, 3], h2T[:, B - 1], start=True, stop=False)
            pe.wait_ge(state_ready, B + 2)
            for t in range(B):
                nc.tensor.matmul(ps_h[t][:], ffn_wT[:, 7], state2[:], start=False, stop=True).then_inc(h_filled, 1)
            for t in range(B):
                pe.wait_ge(hg_ready, t + 1)
                for i in range(NT):
                    last = nc.tensor.transpose(ps_y[t][:, P * i:P * (i + 1)], hg[:, t, P * i:P * (i + 1)], ident[:])
                last.then_inc(y_filled, 1)


_INS = ["L0_attn_x", "L0_attn_WQ", "L0_attn_WK", "L0_attn_WV", "L0_attn_WO", "L0_ffn_wf", "L0_ffn_uf", "L0_ffn_bf",
        "L0_ffn_wi", "L0_ffn_ui", "L0_ffn_bi", "L0_ffn_wc", "L0_ffn_uc", "L0_ffn_bc", "L0_ffn_wo", "L0_ffn_uo",
        "L0_ffn_bo", "L0_ffn_in_c", "L0_c", "L0_wmod"]


def kernel(**inputs):
    import numpy as np
    import concourse.bacc as bacc
    from concourse.bass_utils import run_bass_kernel_spmd

    nc = bacc.Bacc("TRN2", target_bir_lowering=False, num_devices=1)
    arrays, args = {}, []
    for name in _INS:
        a = np.ascontiguousarray(inputs[name])
        arrays[f"in_{name}"] = a
        args.append(nc.dram_tensor(f"in_{name}", a.shape, mybir.dt.from_np(a.dtype), kind="ExternalInput").ap())
    out = nc.dram_tensor("out", (B, S, D), F32, kind="ExternalOutput").ap()
    adaln_block(nc, *args, out)
    r = run_bass_kernel_spmd(nc, [arrays], core_ids=[0])
    return r.results[0]["out"]
```

```python
from contextlib import ExitStack

from concourse import mybir

F32 = mybir.dt.float32
BF16 = mybir.dt.bfloat16
ALU = mybir.AluOpType
ACT = mybir.ActivationFunctionType

P = 128
B, S, D = 4, 512, 128
H = 16
DK = D // H
NT = S // P
HG = 4
GB = H // HG
G = B * GB
NBANK = 10
SCALE = float(DK) ** -0.5
EPS = 1e-5
MASKED = -3.0e38
TWO_ONES = 1.001937866210938

RUNS = ((0, 3), (3, 2), (5, 1))
MAX_ROW = DK * 6
CW = 32

MAX_START = (-2, 8, 18, 29, 39, 49, 60, 70, 80, 90, 100, 110, 120, 130, 140, 150)
EXP_START = (17, 27, 37, 47, 57, 68, 78, 88, 98, 108, 118, 128, 138, 148, 158, 168)
PV_START = (30, 40, 50, 60, 70, 80, 90, 100, 110, 120, 130, 140, 150, 160, 170, 189)
PV_AT = (0, 2, 4, 5)
MAX_PARTS = (2, -4, 9, 8, 8, 12, 10, 11, 11, 12, 12, 8, 8, 12, 9, 10)
MAX_T = (12, 14, 13, 14, 12, 13, 12, 13, 15, 14, 14, 14, 13, 13, 12, 13)
OUT_COPY = (7, 9, 6, 6, 7, 6, 7, 7, 8, 7, 8, 8, 8, 8, 7)
OUT_T = (9, 17, 9, 9, 9, 7, 9, 10, 9, 9, 19, 10, 10, 10, 12)
ONCE = {
    "crow": -63,
    "silu": -58,
    "mod": -49,
    "w_in": -10,
    "w_state": -8,
    "bias": 0,
    "mod2": 38,
    "diag": 41,
    "ga": 48,
}
BATCH = {
    "stat1": (-63, -50, 28, 54),
    "apply1": (-55, -43, 40, 74),
    "aggr1": (-60, -44, 34, 71),
    "lnT1": (-45, -24, 46, 79),
    "q": (-38, -17, 50, 84),
    "mid_q": (-34, -14, 51, 90),
    "k": (-31, -11, 50, 86),
    "mid_k": (-21, -6, 54, 88),
    "stack": (-13, -2, 56, 97),
    "v": (-4, -2, 67, 108),
    "stat2": (79, 116, 158),
    "apply2": (84, 124, 167),
    "attnT": (74, 113, 154),
    "wo": (77, 115, 157),
    "aggr2": (83, 120, 161),
    "lnT2": (88, 129, 169),
    "gate_f": (90, 137, 179),
    "forget": (90, 141, 175),
    "gate_i": (98, 139, 177),
    "gate_c": (99, 139, 180),
    "state": (109, 155, 181),
    "norm": (70, 111, 151, 187),
}


def work_order():
    work = [(t, kind, 0) for kind, t in ONCE.items()]
    for kind, starts in BATCH.items():
        for b, t in enumerate(starts):
            if kind in ("stat1", "stat2", "apply1", "apply2"):
                work += [(t + i, kind, NT * b + i) for i in range(NT)]
            else:
                work.append((t, kind, b))
    for g in range(G):
        work += [(MAX_START[g] + MAX_PARTS[g], "max_parts", g), (MAX_START[g] + MAX_T[g], "maxT", g)]
        if g < G - 1:
            work += [(PV_START[g] + OUT_COPY[g], "out_copy", g), (PV_START[g] + OUT_T[g], "outT", g)]
    return sorted(work, key=lambda w: w[0])


WORK = work_order()
STEPS = range(WORK[0][0], max(WORK[-1][0], PV_START[-1] + PV_AT[-1]) + 1)
SHARED = ("crow", "mod", "mod2", "bias", "w_in", "w_state", "ga", "lnT1", "q", "k", "v", "maxT", "outT", "attnT", "wo", "lnT2",
          "gate_f", "gate_i", "gate_c")
LAST_SHARED = [("last_half0", B - 1), ("last_half1", B - 1)]
SHARED_AT = {w: n for n, w in enumerate([w[1:] for w in WORK if w[1] in SHARED] + LAST_SHARED)}
NORMS = [(w[1][-1], w[2]) for w in WORK if w[1] in ("aggr1", "aggr2")] + [("2", B - 1)]
HALVES = [(slice(c * S // 2, (c + 1) * S // 2), range(c * NT // 2, (c + 1) * NT // 2)) for c in range(2)]


def work_at(t):
    return [w[1:] for w in WORK if w[0] == t]


def attention_at(t, starts):
    return next(((g, t - first) for g, first in enumerate(starts) if first <= t < first + NBANK), None)


def exp_bank(k):
    pair, j = divmod(k, NBANK // 2)
    a, b = 2 * pair, 2 * pair + 1
    return ([(a, 0, 0, 512)], [(b, 0, 0, 512)], [(a, 1, 0, 384), (a, 3, 384, 128)],
            [(b, 1, 0, 384), (b, 3, 384, 128)], [(a, 2, 0, 256), (b, 2, 256, 256)])[j]


def max_bank(k):
    pair, j = divmod(k, NBANK // 2)
    a, b = 2 * pair, 2 * pair + 1
    return ([(a, 3, 0, 512)], [(b, 3, 0, 512)], [(a, 2, 0, 384), (a, 0, 384, 128)],
            [(b, 2, 0, 384), (b, 0, 384, 128)], [(a, 1, 0, 256), (b, 1, 256, 256)])[j]


def strip(h, j):
    return next((k, c0) for k in range(NBANK) for hh, jj, c0, _ in exp_bank(k) if (hh, jj) == (h, j))


def adaln_block(nc, x, WQ, WK, WV, WO, wf, uf, bf, wi, ui, bi, wc, uc, bc, wo, uo, bo, in_c, c, wmod, out):
    ctx = ExitStack()
    with ctx:
        def sb(name, shape, dt=F32):
            return ctx.enter_context(nc.sbuf_tensor(name, shape, dt))

        def sem(name):
            return ctx.enter_context(nc.semaphore(name))

        parts_dram = nc.dram_tensor("parts", [B, 2, 3, DK, H, S], BF16, kind="Internal")

        x_sb = sb("x_sb", [P, B, NT, D])
        x2_sb = sb("x2_sb", [P, B, NT, D])
        w_qkv = sb("w_qkv", [P, 3, D])
        wo_sb = sb("wo_sb", [P, D])
        wo_gated = sb("wo_gated", [P, B, D])
        ffn_w = sb("ffn_w", [P, 8, D])
        ffn_wT = sb("ffn_wT", [P, 8, D])
        wmod_sb = sb("wmod_sb", [P, 6 * D])
        c_rows = sb("c_rows", [B, D])
        c_cols = sb("c_cols", [P, B])
        bias_rows = sb("bias_rows", [5, D])
        bias_cols = sb("bias_cols", [P, 5])
        half_bias = sb("half_bias", [P, 2])
        silu_sb = sb("silu_sb", [P, 3, B])
        mod = sb("mod", [P, 6, B])
        gate_cols = sb("gate_cols", [P, 3, 2, B])
        ga_diag = sb("ga_diag", [P, B, D])
        ones = sb("ones", [P, P])
        ident = sb("ident", [P, P])
        ident_b = sb("ident_b", [P, P], BF16)
        mask = sb("mask", [P, S], BF16)
        
        m_half = sb("m_half", [P, NT])
        two_ones = sb("two_ones", [P, 1])
        stats = sb("stats", [P, 2, NT, 6])
        meanvar = sb("meanvar", [P, 2, NT, 2])
        rstd = sb("rstd", [P, 2, 2, NT])
        z_sb = sb("z_sb", [P, 2, NT, D])
        hT = sb("hT", [P, 2, S])
        h2T = sb("h2T", [P, B, S])
        rem = sb("rem", [P, 2, S])
        parts = sb("parts_sb", [P, 2, 3, S], BF16)
        Qst = sb("Qst", [P, 2, H, S], BF16)
        Kst = sb("Kst", [P, 2, H, S], BF16)
        Vst = sb("Vst", [P, 2, NT, H, CW])
        negm = sb("negm", [P, 2, HG, NT])
        mrest = sb("mrest", [P, HG * NT])
        mparts = sb("mparts", [P, 2, 3, HG * NT], BF16)
        mrow = sb("mrow", [3 * HG * NT, 2, P], BF16)
        Pr = sb("Pr", [P, 2, NBANK, 512])
        oT = sb("oT", [P, 2, S])
        unscaled = sb("unscaled", [P, NT, H, DK + 1])
        recip = sb("recip", [P, NT, H])
        attn = sb("attn", [P, NT, D])
        attnT = sb("attnT", [P, S])
        gates = sb("gates", [P, 3, S])
        fc = sb("fc", [P, S])
        ig = sb("ig", [P, S])
        state2 = sb("state2", [P, S])
        h_out, hg = Pr[:, 0, 0:B], Pr[:, 0, B:2 * B]
        y_sb = Pr[:, 1, 0:B].rearrange("p b (i d) -> p b i d", i=NT)

        def bank(name):
            return ctx.enter_context(nc.psum_tensor(name, [P, 512], F32))

        ps_max = [bank(f"ps_max{n}") for n in range(3)]
        ps_exp = [bank(f"ps_exp{n}") for n in range(2)]
        ps_out = bank("ps_out")
        ps_shared = [bank(f"ps_shared{n}") for n in range(2)]
        ps_half = [ps_shared[SHARED_AT[kind, B - 1] % 2] for kind in ("last_half0", "last_half1")]
        ps_gate = ps_max
        ps_piece = [*ps_exp, ps_out, *ps_half, *ps_max]

        x_in = [sem(f"x_in{b}") for b in range(B)]
        c_in, bias_in, wmod_in, w_in, ffnw_in, wo_in = (sem(n) for n in ("c_in", "bias_in", "wmod_in", "w_in", "ffnw_in", "wo_in"))
        ident_made, consts_made, qst_clear, kst_set, v_ones = (
            sem(n) for n in ("ident_made", "consts_made", "qst_clear", "kst_set", "v_ones"))
        shared_filled = sem("shared_filled")
        shared_drained = [sem("shared_drained0"), sem("shared_drained1")]
        max_filled, max_drained = sem("max_filled"), sem("max_drained")
        exp_filled, exp_drained = sem("exp_filled"), sem("exp_drained")
        masked = sem("masked")
        out_filled, out_drained, attn_ready = sem("out_filled"), sem("out_drained"), sem("attn_ready")
        max_split, mrow_stored = sem("max_split"), [sem("mrow_in0"), sem("mrow_in1")]
        parts_hi, parts_mid, parts_lo = sem("parts_hi"), sem("parts_mid"), sem("parts_lo")
        parts_out = [[sem(f"parts_out_{o}{p}") for p in range(3)] for o in "qk"]
        stack_in = [sem("stack_in0"), sem("stack_in1")]
        first_heads_in = sem("first_heads_in")
        ln_tile, ln_stats, ln_rstd, ln_z = (sem(n) for n in ("ln_tile", "ln_stats", "ln_rstd", "ln_z"))
        silu_tanh, silu_ready, gate_copied = sem("silu_tanh"), sem("silu_ready"), sem("gate_copied")
        gates_floored, diag_ready = sem("gates_floored"), sem("diag_ready")
        state_ready, forget_ready = sem("state_ready"), sem("forget_ready")
        last_outT, last_attn, last_attnT, last_attnT_copied, last_wo, last_x2, last_lnT, last_h2T = (sem(n) for n in (
            "last_outT", "last_attn", "last_attnT", "last_attnT_copied", "last_wo", "last_x2", "last_lnT", "last_h2T"))
        gate_filled, gate_ready = sem("gate_filled"), sem("gate_ready")
        pair_made, ones_made = sem("pair_made"), sem("ones_made")
        h_filled, h_ready, hg_ready, y_filled, y_ready, y_out = (
            sem(n) for n in ("h_filled", "h_ready", "hg_ready", "y_filled", "y_ready", "y_out"))
        dve_step, pool_step, act_step = sem("dve_step"), sem("pool_step"), sem("act_step")

        def wait_filled(eng, kind, n):
            eng.wait_ge(shared_filled, SHARED_AT[kind, n] + 1)

        def shared_bank(kind, n):
            return ps_shared[SHARED_AT[kind, n] % 2]

        def drained_by(kind, n):
            return shared_drained[SHARED_AT[kind, n] % 2]

        def wait_drained(eng, kind, n):
            eng.wait_ge(drained_by(kind, n), SHARED_AT[kind, n] // 2 + 1)

        def stacks_loaded(b):
            return 16 * (6 * (b // 2 + 1) + b // 2)

        def stacks_ready(eng, g):
            b = g // GB
            if g == 0:
                eng.wait_ge(first_heads_in, 16 * 6)
            else:
                eng.wait_ge(stack_in[b % 2], stacks_loaded(b))

        block = ctx.enter_context(nc.Block())

        @block.sync
        def _(sp):
            def store_part(b, op, part):
                sp.wait_ge((parts_hi, parts_mid, parts_lo)[part], 2 * b + op + 1)
                sp.dma_start(parts_dram[b, op, part].rearrange("d h s -> h d s"), parts[:, op, part]).then_inc(parts_out[op][part], 16)

            def load_run(b, op, run, h0, h1, done):
                t, many = RUNS[run]
                rows, part = slice(DK * t, DK * (t + many)), run if op == 0 else many - 1
                sp.wait_ge(parts_out[op][part], 16 * (b + 1))
                if op == 0:
                    src = parts_dram[b, 0, run, :, h0:h1].rearrange("d h s -> d (h s)").unsqueeze(0).broadcast_to([many, DK, (h1 - h0) * S])
                else:
                    src = parts_dram[b, 1, 0:many, :, h0:h1].rearrange("t d h s -> (t d) (h s)")
                sp.dma_start((Qst, Kst)[op][rows, b % 2, h0:h1], src).then_inc(done, 16)

            sp.dma_start(x_sb[:, 0], x[0].rearrange("(i p) d -> p i d", p=P)).then_inc(x_in[0], 16)
            for n, w in enumerate((WQ, WK, WV)):
                sp.dma_start(w_qkv[:, n], w[:, :]).then_inc(w_in, 16)
            sp.dma_start(x_sb[:, 1], x[1].rearrange("(i p) d -> p i d", p=P)).then_inc(x_in[1], 16)
            sp.dma_start(wo_sb[:], WO[:, :]).then_inc(wo_in, 16)
            for n, v in enumerate((bf, bi, bc, bo, in_c)):
                sp.dma_start(bias_rows[n:n + 1, :], v.rearrange("(a n) -> a n", a=1)).then_inc(bias_in, 16)
            for i, w in enumerate((wf, wi, wc, wo, uf, ui, uc, uo)):
                sp.dma_start(ffn_w[:, i], w[:, :]).then_inc(ffnw_in, 16)
            for t in STEPS:
                for kind, n in work_at(t):
                    if kind == "stack":
                        for part in range(3):
                            store_part(n, 0, part)
                        if n == 1:
                            for b in range(2, B):
                                sp.dma_start(x_sb[:, b], x[b].rearrange("(i p) d -> p i d", p=P)).then_inc(x_in[b], 16)
                        for part in range(3):
                            store_part(n, 1, part)
                        if n < 2:
                            sp.wait_ge(qst_clear, n + 1)
                            sp.wait_ge(kst_set, n + 1)
                        else:
                            sp.wait_ge(exp_filled, NBANK * GB * (n - 1))
                            sp.dma_start(Qst[MAX_ROW:MAX_ROW + 3, n % 2], Qst[96:99, n % 2]).then_inc(stack_in[n % 2], 16)
                        first, done = (HG, first_heads_in) if n == 0 else (H, stack_in[n % 2])
                        for op, run in ((0, 0), (0, 1), (0, 2), (1, 2), (1, 1), (1, 0)):
                            load_run(n, op, run, 0, first, done)
                        if n == 0:
                            for op, run in ((0, 0), (0, 1), (0, 2), (1, 2), (1, 1), (1, 0)):
                                load_run(n, op, run, first, H, stack_in[0])
                    elif kind == "maxT":
                        wait_drained(sp, "maxT", n)
                        if n >= 2:
                            sp.wait_ge(mrow_stored[n % 2], 16 * (n // 2))
                        b, h = n // GB, HG * (n % GB)
                        sp.dma_start(Qst[MAX_ROW:MAX_ROW + 3, b % 2, h:h + HG, :], mrow[:, n % 2]).then_inc(mrow_stored[n % 2], 16)
            for c, (_, tiles) in enumerate(HALVES):
                for b in range(B):
                    sp.wait_ge(y_ready, B * c + b + 1)
                    i0, i1 = tiles[0], tiles[-1] + 1
                    sp.dma_start(out[b, P * i0:P * i1].rearrange("(i p) d -> p i d", p=P), y_sb[:, b, i0:i1]).then_inc(y_out, 16)
            sp.wait_ge(y_out, 16 * 2 * B)

        @block.gpsimd
        def _(pool):
            steps = [0]

            def link(ins):
                steps[0] += 1
                ins.then_inc(pool_step, 1)
                pool.wait_ge(pool_step, steps[0])

            nc.gpsimd.memset(two_ones[:], TWO_ONES).then_inc(pair_made, 1)
            link(nc.gpsimd.memset(ident[:], 0.0))
            nc.gpsimd.affine_select(out=ident[:], in_=ident[:], compare_op=ALU.not_equal, fill=1.0, base=0,
                                    pattern=[[-1, P]], channel_multiplier=1).then_inc(ident_made, 1)
            nc.gpsimd.memset(Qst[:, 0].rearrange("p h s -> p (h s)").bitcast(F32), 0.0).then_inc(qst_clear, 1)
            nc.gpsimd.memset(ones[:], 1.0).then_inc(ones_made, 1)
            link(nc.gpsimd.memset(m_half[:], -0.5))
            for t in STEPS:
                for kind, n in work_at(t):
                    if kind in ("aggr1", "aggr2"):
                        m = NORMS.index((kind[-1], n))
                        pool.wait_ge(ln_stats, m + 1)
                        link(nc.gpsimd.tensor_scalar(rstd[:, m % 2, 0], meanvar[:, m % 2, :, 1], EPS, None, ALU.add))
                        nc.gpsimd.tensor_tensor(out=rstd[:, m % 2, 1], in0=rstd[:, m % 2, 0], in1=m_half[:],
                                                op=ALU.pow).then_inc(ln_rstd, 1)
                        if (kind, n) == ("aggr1", 0):
                            link(nc.gpsimd.memset(mask[:], 0.0))
                            nc.gpsimd.tensor_copy(ident_b[:], ident[:])
                            nc.gpsimd.affine_select(out=mask[:], in_=mask[:], compare_op=ALU.is_ge, fill=MASKED, base=S - P,
                                                    pattern=[[-1, S]], channel_multiplier=1).then_inc(consts_made, 1)
                        elif (kind, n) == ("aggr1", 1):
                            nc.gpsimd.memset(Qst[:, 1].rearrange("p h s -> p (h s)").bitcast(F32), 0.0).then_inc(qst_clear, 1)
                            nc.gpsimd.memset(Kst[:, 1].rearrange("p h s -> p (h s)").bitcast(F32), TWO_ONES).then_inc(kst_set, 1)
                            link(nc.gpsimd.memset(Vst[:], 0.0))
                            nc.gpsimd.memset(Vst[:, :, :, :, DK:DK + 1], 1.0).then_inc(v_ones, 1)
                    elif kind in ("mid_q", "mid_k") and n >= 2:
                        op = "qk".index(kind[-1])
                        pool.wait_ge(parts_mid, 2 * n + op + 1)
                        nc.gpsimd.tensor_tensor(out=parts[:, op, 2], in0=rem[:, op], in1=parts[:, op, 1],
                                                op=ALU.subtract).then_inc(parts_lo, 1)
                    elif kind == "max_parts":
                        pool.wait_ge(max_drained, NBANK * (n + 1))
                        if n >= 2:
                            wait_filled(pool, "maxT", n - 2)
                        if n:
                            pool.wait_ge(max_split, n)
                        m, mp = negm[:, n % 2].rearrange("p h i -> p (h i)"), mparts[:, n % 2]
                        link(nc.gpsimd.tensor_copy(mp[:, 0], m))
                        link(nc.gpsimd.tensor_tensor(out=mrest[:], in0=m, in1=mp[:, 0], op=ALU.subtract))
                        link(nc.gpsimd.tensor_copy(mp[:, 1], mrest[:]))
                        nc.gpsimd.tensor_tensor(out=mp[:, 2], in0=mrest[:], in1=mp[:, 1], op=ALU.subtract).then_inc(max_split, 1)
                at = attention_at(t, EXP_START)
                if at and at[1] % 5 == 4:
                    g, k = at
                    pool.wait_ge(exp_drained, NBANK * g + k + 1)
                    first = Pr[:, g % 2, k - 4:k]
                    for blocks in (first[:, :, 0:P], first[:, 2:4, 384:512],
                                   Pr[:, g % 2, k].rearrange("p (h q) -> p h q", h=2)[:, :, 0:P]):
                        last = nc.gpsimd.affine_select(out=blocks, in_=blocks, compare_op=ALU.is_ge, fill=0.0, base=0,
                                                       pattern=[[0, blocks.shape[1]], [1, P]], channel_multiplier=-1)
                    last.then_inc(masked, 1)
            m = len(NORMS) - 1
            for c, (_, tiles) in enumerate(HALVES):
                pool.wait_ge(ln_stats, m + c + 1)
                i0, i1 = tiles[0], tiles[-1] + 1
                link(nc.gpsimd.tensor_scalar(rstd[:, m % 2, 0, i0:i1], meanvar[:, m % 2, i0:i1, 1], EPS, None, ALU.add))
                nc.gpsimd.tensor_tensor(out=rstd[:, m % 2, 1, i0:i1], in0=rstd[:, m % 2, 0, i0:i1], in1=m_half[:, i0:i1],
                                        op=ALU.pow).then_inc(ln_rstd, 1)

        @block.scalar
        def _(act):
            def tanh_gate(out_, src, i):
                return nc.scalar.activation(out_, src, ACT.Tanh, scale=0.5 if i < 2 else 1.0,
                                            bias=half_bias[:, i:i + 1] if i < 2 else bias_cols[:, 2:3])

            act.dma_start(c_rows[:], c[:, :]).then_inc(c_in, 16)
            act.dma_start(wmod_sb[:], wmod[:, :]).then_inc(wmod_in, 16)
            nc.scalar.preload_act_table(ACT.Exp)

            for t in STEPS:
                for kind, n in work_at(t):
                    if kind == "out_copy":
                        act.wait_ge(out_filled, n + 1)
                        if n >= 2:
                            wait_filled(act, "outT", n - 2)
                        nc.scalar.activation(oT[:, n % 2], ps_out[:], ACT.Copy).then_inc(out_drained, 1)
                    if kind in ("mid_q", "mid_k") and n >= 2:
                        op = "qk".index(kind[-1])
                        wait_drained(act, kind[-1], n)
                        act.wait_ge(parts_out[op][1], 16 * n)
                        act.wait_ge(parts_out[op][2], 16 * n)
                        nc.scalar.activation(parts[:, op, 1], rem[:, op], ACT.Copy).then_inc(parts_mid, 1)
                    if kind == "diag":
                        act.wait_ge(gates_floored, 1)
                        for b in range(B):
                            last = nc.scalar.activation(ga_diag[:, b], ident[:], ACT.Copy, scale=gate_cols[:, 2, 0, b:b + 1])
                        last.then_inc(diag_ready, 1)
                    if kind not in SHARED or kind in ("mod", "mod2", "ga", "wo"):
                        continue
                    src, done = shared_bank(kind, n), drained_by(kind, n)
                    wait_filled(act, kind, n)
                    if kind == "crow":
                        nc.scalar.activation(c_cols[:], src[:, 0:B], ACT.Copy).then_inc(done, 1)
                        wait_drained(act, kind, n)
                        nc.scalar.activation(silu_sb[:, 0], c_cols[:], ACT.Tanh, scale=0.5).then_inc(silu_tanh, 1)
                        act.wait_ge(pair_made, 1)
                        nc.scalar.activation(Kst[:, 0].rearrange("p h s -> p (h s)").bitcast(F32),
                                             two_ones[:, 0:1].broadcast_to([P, H * S // 2]), ACT.Copy).then_inc(kst_set, 1)
                    elif kind == "bias":
                        nc.scalar.activation(bias_cols[:], src[:, 0:5], ACT.Copy).then_inc(done, 1)
                        wait_drained(act, kind, n)
                        nc.scalar.activation(half_bias[:], bias_cols[:, 0:2], ACT.Copy, scale=0.5).then_inc(act_step, 1)
                        nc.scalar.activation(state2[:], bias_cols[:, 4:5].broadcast_to([P, S]), ACT.Copy, scale=2.0).then_inc(state_ready, 1)
                    elif kind == "w_in":
                        nc.scalar.activation(ffn_wT[:, 0:4].rearrange("p n m -> p (n m)"), src[:], ACT.Copy).then_inc(done, 1)
                    elif kind == "w_state":
                        nc.scalar.activation(ffn_wT[:, 4:8].rearrange("p n m -> p (n m)"), src[:], ACT.Copy, scale=0.5).then_inc(done, 1)
                    elif kind == "lnT1":
                        wait_drained(act, "mod", 0)
                        if n >= 2:
                            wait_filled(act, "v", n - 2)
                        nc.scalar.activation(hT[:, n % 2], src[:], ACT.Identity, scale=mod[:, 1, n:n + 1],
                                             bias=mod[:, 0, n:n + 1]).then_inc(done, 1)
                    elif kind in ("q", "k"):
                        op = "qk".index(kind)
                        if n:
                            act.wait_ge(parts_out[op][0], 16 * n)
                        nc.scalar.activation(parts[:, op, 0], src[:], ACT.Copy).then_inc(parts_hi, 1)
                    elif kind == "v":
                        act.wait_ge(v_ones, 1)
                        if n >= 2:
                            act.wait_ge(out_filled, GB * (n - 1))
                        nc.scalar.activation(Vst[:, n % 2, :, :, 0:DK], src[:].rearrange("p (i h d) -> p i h d", i=NT, d=DK),
                                             ACT.Copy).then_inc(done, 1)
                    elif kind == "maxT":
                        if n >= 2:
                            act.wait_ge(mrow_stored[n % 2], 16 * (n // 2))
                        nc.scalar.activation(mrow[:, n % 2], src[0:3 * HG * NT, 0:P // 2].bitcast(BF16), ACT.Copy).then_inc(done, 1)
                    elif kind == "outT":
                        if n >= GB:
                            act.wait_ge(attn_ready, n // GB)
                        h = HG * (n % GB)
                        nc.scalar.activation(unscaled[:, :, h:h + HG], src[:].rearrange("p (i h v) -> p i h v", i=NT, v=CW)[:, :, :, 0:DK + 1],
                                             ACT.Copy).then_inc(done, 1)
                    elif kind == "attnT":
                        if n:
                            wait_filled(act, "wo", n - 1)
                        nc.scalar.activation(attnT[:], src[:], ACT.Copy).then_inc(done, 1)
                    elif kind == "lnT2":
                        wait_drained(act, "mod2", 0)
                        nc.scalar.activation(h2T[:, n], src[:], ACT.Identity, scale=mod[:, 4, n:n + 1],
                                             bias=mod[:, 3, n:n + 1]).then_inc(done, 1)
                    else:
                        i = "fic".index(kind[-1])
                        if (kind, n) == ("gate_f", 0):
                            act.wait_ge(act_step, 1)
                        act.wait_ge(state_ready, n + 1)
                        tanh_gate(gates[:, i], src[:], i).then_inc(done, 1)
                at = attention_at(t, EXP_START)
                if at:
                    g, k = at
                    if k == 0 and g >= 2:
                        act.wait_ge(out_filled, g - 1)
                    act.wait_ge(exp_filled, NBANK * g + k + 1)
                    nc.scalar.activation(Pr[:, g % 2, k], ps_exp[(NBANK * g + k) % 2][:], ACT.Exp, scale=SCALE).then_inc(exp_drained, 1)
            n = B - 1
            act.wait_ge(out_filled, G)
            wait_filled(act, "outT", G - 3)
            for cols, _ in HALVES:
                nc.scalar.activation(oT[:, (G - 1) % 2, cols], ps_out[:, cols], ACT.Copy).then_inc(out_drained, 1)
            for half, (cols, _) in enumerate(HALVES):
                act.wait_ge(last_attnT, half + 1)
                if half == 0:
                    wait_filled(act, "wo", n - 1)
                nc.scalar.activation(attnT[:, cols], ps_half[half][:, cols], ACT.Copy).then_inc(last_attnT_copied, 1)
            for half, (cols, _) in enumerate(HALVES):
                act.wait_ge(last_lnT, half + 1)
                nc.scalar.activation(h2T[:, n, cols], ps_half[half][:, cols], ACT.Identity, scale=mod[:, 4, n:n + 1],
                                     bias=mod[:, 3, n:n + 1]).then_inc(last_h2T, 1)
            act.wait_ge(state_ready, B)
            for i in range(3):
                act.wait_ge(gate_filled, i + 1)
                for cols in [slice(0, S)] if i < 2 else [cols for cols, _ in HALVES]:
                    tanh_gate(gates[:, i, cols], ps_gate[i][:, cols], i).then_inc(gate_ready, 1)
            for half, (cols, _) in enumerate(HALVES):
                for t in range(B):
                    act.wait_ge(h_filled, B * half + t + 1)
                    nc.scalar.activation(h_out[:, t, cols], ps_piece[B * half + t][:, cols], ACT.Tanh, bias=bias_cols[:, 3:4]).then_inc(h_ready, 1)

        @block.vector
        def _(dve):
            steps = [0]

            def link(ins):
                steps[0] += 1
                ins.then_inc(dve_step, 1)
                dve.wait_ge(dve_step, steps[0])

            def signed_floor(out_, gate, sign, magnitude):
                link(nc.vector.tensor_scalar(sign, gate, 0.0, 2.0, ALU.is_ge, ALU.mult))
                link(nc.vector.scalar_tensor_tensor(out=magnitude, in0=gate, scalar=-1.0, in1=gate, op0=ALU.mult, op1=ALU.max))
                link(nc.vector.tensor_scalar(magnitude, magnitude, 0.25, None, ALU.max))
                nc.vector.scalar_tensor_tensor(out=out_, in0=sign, scalar=1.0, in1=magnitude, op0=ALU.subtract,
                                               op1=ALU.mult).then_inc(gates_floored, 1)

            def times_forget(cols=slice(0, S)):
                nc.vector.scalar_tensor_tensor(out=fc[:, cols], in0=gates[:, 0, cols], scalar=1.0, in1=state2[:, cols],
                                               op0=ALU.add, op1=ALU.mult).then_inc(forget_ready, 1)

            def new_state(forgotten, cols=slice(0, S)):
                link(nc.vector.scalar_tensor_tensor(out=ig[:, cols], in0=gates[:, 1, cols], scalar=1.0, in1=gates[:, 2, cols],
                                                    op0=ALU.add, op1=ALU.mult))
                dve.wait_ge(forget_ready, forgotten)
                nc.vector.scalar_tensor_tensor(out=state2[:, cols], in0=fc[:, cols], scalar=0.5, in1=ig[:, cols], op0=ALU.mult,
                                               op1=ALU.add).then_inc(state_ready, 1)

            def normalise(products, heads, tiles, done):
                r = recip[:, tiles, heads]
                shape = [P, *r.shape[1:], DK]
                link(nc.vector.reciprocal(r, products[:, :, :, DK]))
                nc.vector.tensor_tensor(out=attn[:, tiles].rearrange("p i (h v) -> p i h v", v=DK)[:, :, heads],
                                        in0=products[:, :, :, 0:DK], in1=r.unsqueeze(3).broadcast_to(shape),
                                        op=ALU.mult).then_inc(done, 1)

            for t in STEPS:
                for kind, n in work_at(t):
                    if kind in ("mod", "mod2", "ga", "wo"):
                        wait_filled(dve, kind, n)
                        src, done = shared_bank(kind, n), drained_by(kind, n)
                    if kind == "silu":
                        dve.wait_ge(silu_tanh, 1)
                        link(nc.vector.scalar_tensor_tensor(out=silu_sb[:, 1], in0=silu_sb[:, 0], scalar=1.0, in1=c_cols[:],
                                                            op0=ALU.add, op1=ALU.mult))
                        nc.vector.tensor_scalar(silu_sb[:, 2], silu_sb[:, 1], 0.5, None, ALU.mult).then_inc(silu_ready, 1)
                    elif kind in ("mod", "mod2"):
                        m = 0 if kind == "mod" else 3
                        cols = src[:, 0:6 * B].rearrange("p (m b) -> p m b", m=6)
                        nc.vector.tensor_scalar(mod[:, m + 1], cols[:, m + 1], 1.0, None, ALU.add)
                        if kind == "mod2":
                            nc.vector.tensor_copy(mod[:, 2:6:3], cols[:, 2:6:3]).then_inc(gate_copied, 1)
                        nc.vector.tensor_copy(mod[:, m], cols[:, m]).then_inc(done, 1)
                        if kind == "mod2":
                            dve.wait_ge(gate_copied, 1)
                            signed_floor(gate_cols[:, 2], mod[:, 2:6:3], gate_cols[:, 0], gate_cols[:, 1])
                    elif kind == "ga":
                        dve.wait_ge(wo_in, 16)
                        nc.vector.tensor_tensor(out=wo_gated[:], in0=src[:].rearrange("p (b d) -> p b d", b=B),
                                                in1=wo_sb[:].unsqueeze(1).broadcast_to([P, B, D]), op=ALU.mult).then_inc(done, 1)
                    elif kind in ("stat1", "stat2"):
                        b, i = divmod(n, NT)
                        m = NORMS.index((kind[-1], b))
                        if i == 0 and kind == "stat1":
                            dve.wait_ge(x_in[b], 16)
                        if i == 0 and kind == "stat2":
                            wait_drained(dve, "wo", b)
                        if i == 0 and m >= 2:
                            dve.wait_ge(ln_rstd, m - 1)
                        src = x_sb if kind == "stat1" else x2_sb
                        nc.vector.bn_stats(stats[:, m % 2, i], src[:, b, i]).then_inc(ln_tile, 1)
                    elif kind in ("aggr1", "aggr2"):
                        m = NORMS.index((kind[-1], n))
                        dve.wait_ge(ln_tile, NT * (m + 1))
                        for i in range(NT):
                            last = nc.vector.bn_aggr(meanvar[:, m % 2, i], stats[:, m % 2, i])
                        last.then_inc(ln_stats, 1)
                    elif kind in ("apply1", "apply2"):
                        b, i = divmod(n, NT)
                        m = NORMS.index((kind[-1], b))
                        src = x_sb if kind == "apply1" else x2_sb
                        if i == 0:
                            dve.wait_ge(ln_rstd, m + 1)
                            if m >= 2:
                                wait_filled(dve, "lnT" + NORMS[m - 2][0], NORMS[m - 2][1])
                        nc.vector.tensor_scalar(z_sb[:, m % 2, i], src[:, b, i], meanvar[:, m % 2, i, 0:1],
                                                rstd[:, m % 2, 1, i:i + 1], ALU.subtract, ALU.mult).then_inc(ln_z, 1)
                    elif kind in ("q", "k"):
                        op = "qk".index(kind)
                        dve.wait_ge(parts_hi, 2 * n + op + 1)
                        if n:
                            dve.wait_ge(parts_lo, 2 * n)
                        nc.vector.tensor_tensor(out=rem[:, op], in0=shared_bank(kind, n)[:], in1=parts[:, op, 0],
                                                op=ALU.subtract).then_inc(drained_by(kind, n), 1)
                    elif kind in ("mid_q", "mid_k") and n < 2:
                        op = "qk".index(kind[-1])
                        wait_drained(dve, kind[-1], n)
                        if n:
                            dve.wait_ge(parts_out[op][1], 16 * n)
                            dve.wait_ge(parts_out[op][2], 16 * n)
                        nc.vector.tensor_copy(parts[:, op, 1], rem[:, op]).then_inc(parts_mid, 1)
                        dve.wait_ge(parts_mid, 2 * n + op + 1)
                        nc.vector.tensor_tensor(out=parts[:, op, 2], in0=rem[:, op], in1=parts[:, op, 1],
                                                op=ALU.subtract).then_inc(parts_lo, 1)
                    elif kind == "norm":
                        heads = H if n < B - 1 else H - HG
                        for g in range(GB * n, GB * n + heads // HG):
                            wait_drained(dve, "outT", g)
                        if n:
                            wait_filled(dve, "attnT", n - 1)
                            dve.wait_ge(attn_ready, n)
                        normalise(unscaled[:, :, 0:heads], slice(0, heads), slice(0, NT), attn_ready)
                    elif kind == "wo":
                        nc.vector.tensor_tensor(out=x2_sb[:, n].rearrange("p i d -> p (i d)"), in0=src[:],
                                                in1=x_sb[:, n].rearrange("p i d -> p (i d)"), op=ALU.add).then_inc(done, 1)
                    elif kind == "forget":
                        dve.wait_ge(state_ready, n + 1)
                        wait_drained(dve, "gate_f", n)
                        times_forget()
                    elif kind == "state":
                        wait_drained(dve, "gate_i", n)
                        wait_drained(dve, "gate_c", n)
                        new_state(n + 1)
                at = attention_at(t, MAX_START)
                if at:
                    g, k = at
                    if k == 0 and g == 0:
                        dve.wait_ge(consts_made, 1)
                    if k == 0 and g >= 2:
                        dve.wait_ge(max_split, g - 1)
                    dve.wait_ge(max_filled, NBANK * g + k + 1)
                    pb = ps_max[(NBANK * g + k) % 3]
                    m = negm[:, g % 2]
                    for h, i, c0, w in max_bank(k):
                        last = nc.vector.tensor_tensor_reduce(
                            out=pb[:, c0:c0 + w], in0=pb[:, c0:c0 + w], in1=mask[:, S - w:S], scale=-1.0, scalar=-MASKED,
                            op0=ALU.add, op1=ALU.min, accum_out=m[:, h, i:i + 1])
                    last.then_inc(max_drained, 1)
            n, m = B - 1, len(NORMS) - 1
            for c, (_, tiles) in enumerate(HALVES):
                dve.wait_ge(last_outT, c + 1)
                if c == 0:
                    dve.wait_ge(attn_ready, B)
                i = slice(tiles[0], tiles[-1] + 1)
                normalise(ps_half[c][:].rearrange("p (i h v) -> p i h v", i=NT, v=CW)[:, i], slice(H - HG, H), i, last_attn)
            dve.wait_ge(ln_rstd, m - 1)
            for c, (cols, tiles) in enumerate(HALVES):
                dve.wait_ge(last_wo, c + 1)
                for i in tiles:
                    last = nc.vector.tensor_tensor(out=x2_sb[:, n, i], in0=ps_half[c][:, P * i:P * (i + 1)], in1=x_sb[:, n, i], op=ALU.add)
                last.then_inc(last_x2, 1)
                dve.wait_ge(last_x2, c + 1)
                for i in tiles:
                    last = nc.vector.bn_stats(stats[:, m % 2, i], x2_sb[:, n, i])
                link(last)
                for i in tiles:
                    last = nc.vector.bn_aggr(meanvar[:, m % 2, i], stats[:, m % 2, i])
                last.then_inc(ln_stats, 1)
            wait_filled(dve, "lnT" + NORMS[m - 2][0], NORMS[m - 2][1])
            for c, (_, tiles) in enumerate(HALVES):
                dve.wait_ge(ln_rstd, m + c + 1)
                for i in tiles:
                    nc.vector.tensor_scalar(z_sb[:, m % 2, i], x2_sb[:, n, i], meanvar[:, m % 2, i, 0:1],
                                            rstd[:, m % 2, 1, i:i + 1], ALU.subtract, ALU.mult).then_inc(ln_z, 1)
            dve.wait_ge(state_ready, B)
            dve.wait_ge(gate_ready, 1)
            times_forget()
            for c, (cols, _) in enumerate(HALVES):
                dve.wait_ge(gate_ready, c + 3)
                new_state(B, cols)
            pieces = [(c, t) for c in range(2) for t in range(B)]
            for k in range(len(pieces) + 2):
                if k < len(pieces):
                    c, t = pieces[k]
                    cols = HALVES[c][0]
                    dve.wait_ge(h_ready, k + 1)
                    nc.vector.tensor_scalar(hg[:, t, cols], h_out[:, t, cols], gate_cols[:, 2, 1, t:t + 1], None, ALU.mult).then_inc(hg_ready, 1)
                if k >= 2:
                    c, t = pieces[k - 2]
                    cols, tiles = HALVES[c]
                    i0, i1 = tiles[0], tiles[-1] + 1
                    dve.wait_ge(y_filled, k - 1)
                    nc.vector.tensor_tensor(out=y_sb[:, t, i0:i1].rearrange("p i d -> p (i d)"), in0=ps_piece[k - 2][:, cols],
                                            in1=x2_sb[:, t, i0:i1].rearrange("p i d -> p (i d)"), op=ALU.add).then_inc(y_ready, 1)

        @block.tensor
        def _(pe):
            def fills(ins):
                ins.then_inc(shared_filled, 1)

            def take_shared(kind, n):
                at = SHARED_AT[kind, n]
                if at >= 2:
                    pe.wait_ge(shared_drained[at % 2], at // 2)
                return shared_bank(kind, n)

            def transpose_norm(which, n):
                m = NORMS.index((which, n))
                pb = take_shared("lnT" + which, n)
                for i in range(NT):
                    pe.wait_ge(ln_z, NT * m + i + 1)
                    last = nc.tensor.transpose(pb[:, P * i:P * (i + 1)], z_sb[:, m % 2, i], ident[:])
                fills(last)

            for t in STEPS:
                at = attention_at(t, MAX_START)
                if at:
                    g, k = at
                    b, h0 = g // GB, HG * (g % GB)
                    if k == 0:
                        stacks_ready(pe, g)
                    n = NBANK * g + k
                    if n >= 3:
                        pe.wait_ge(max_drained, n - 2)
                    pb = ps_max[n % 3]
                    for h, i, c0, w in max_bank(k):
                        last = nc.tensor.matmul(pb[:, c0:c0 + w], Qst[:, b % 2, h0 + h, P * i:P * (i + 1)], Kst[:, b % 2, h0 + h, 0:w],
                                                start=True, stop=True)
                    last.then_inc(max_filled, 1)
                for kind, n in work_at(t):
                    if kind not in SHARED:
                        continue
                    if kind in ("lnT1", "lnT2"):
                        transpose_norm(kind[-1], n)
                        continue
                    pb = take_shared(kind, n)
                    if kind == "crow":
                        pe.wait_ge(ident_made, 1)
                        pe.wait_ge(c_in, 16)
                        fills(nc.tensor.transpose(pb[:, 0:B], c_rows[:, :], ident[0:B, 0:B]))
                    elif kind == "bias":
                        pe.wait_ge(bias_in, 16 * 5)
                        fills(nc.tensor.transpose(pb[:, 0:5], bias_rows[:, :], ident[0:5, 0:5]))
                    elif kind in ("w_in", "w_state"):
                        pe.wait_ge(ffnw_in, 16 * 8)
                        for i in range(4):
                            last = nc.tensor.transpose(pb[:, P * i:P * (i + 1)], ffn_w[:, 4 * (kind == "w_state") + i], ident[:])
                        fills(last)
                    elif kind in ("mod", "mod2"):
                        pe.wait_ge(silu_ready, 1)
                        pe.wait_ge(wmod_in, 16)
                        for m in (0, 1) if kind == "mod" else (2, 3, 4, 5):
                            last = nc.tensor.matmul(pb[:, m * B:(m + 1) * B], wmod_sb[:, m * D:(m + 1) * D], silu_sb[:, 2], start=True, stop=True)
                        fills(last)
                    elif kind == "ga":
                        pe.wait_ge(diag_ready, 1)
                        pe.wait_ge(ones_made, 1)
                        fills(nc.tensor.matmul(pb[:], ones[:], ga_diag[:].rearrange("p b d -> p (b d)"), start=True, stop=True))
                    elif kind in ("q", "k"):
                        wait_drained(pe, "lnT1", n)
                        pe.wait_ge(w_in, 16 * 3)
                        fills(nc.tensor.matmul(pb[:], w_qkv[:, "qk".index(kind)], hT[:, n % 2], start=True, stop=True))
                    elif kind == "v":
                        for i in range(NT):
                            last = nc.tensor.matmul(pb[:, P * i:P * (i + 1)], hT[:, n % 2, P * i:P * (i + 1)], w_qkv[:, 2], start=True, stop=True)
                        fills(last)
                    elif kind == "maxT":
                        pe.wait_ge(max_split, n + 1)
                        fills(nc.tensor.transpose(pb[0:3 * HG * NT, 0:P // 2].bitcast(BF16),
                                                  mparts[:, n % 2].rearrange("p t m -> p (t m)"), ident_b[:]))
                    elif kind == "outT":
                        pe.wait_ge(out_drained, n + 1)
                        for i in range(NT):
                            last = nc.tensor.transpose(pb[:, P * i:P * (i + 1)], oT[:, n % 2, P * i:P * (i + 1)], ident[:])
                        fills(last)
                    elif kind == "attnT":
                        pe.wait_ge(attn_ready, n + 1)
                        for i in range(NT):
                            last = nc.tensor.transpose(pb[:, P * i:P * (i + 1)], attn[:, i], ident[:])
                        fills(last)
                    elif kind == "wo":
                        wait_drained(pe, "attnT", n)
                        wait_drained(pe, "ga", 0)
                        for i in range(NT):
                            last = nc.tensor.matmul(pb[:, P * i:P * (i + 1)], attnT[:, P * i:P * (i + 1)], wo_gated[:, n], start=True, stop=True)
                        fills(last)
                    else:
                        i = "fic".index(kind[-1])
                        pe.wait_ge(state_ready, n + 1)
                        if (kind, n) == ("gate_f", 0):
                            wait_drained(pe, "w_in", 0)
                            wait_drained(pe, "w_state", 0)
                        nc.tensor.matmul(pb[:], ffn_wT[:, 4 + i], state2[:], start=True, stop=False)
                        wait_drained(pe, "lnT2", n)
                        fills(nc.tensor.matmul(pb[:], ffn_wT[:, i], h2T[:, n], start=False, stop=True))
                at = attention_at(t, EXP_START)
                if at:
                    g, k = at
                    b, h0 = g // GB, HG * (g % GB)
                    if k == 0:
                        pe.wait_ge(mrow_stored[g % 2], 16 * (g // 2 + 1))
                    n = NBANK * g + k
                    if n >= 2:
                        pe.wait_ge(exp_drained, n - 1)
                    for h, j, c0, w in exp_bank(k):
                        last = nc.tensor.matmul(ps_exp[n % 2][:, c0:c0 + w], Kst[:, b % 2, h0 + h, P * j:P * (j + 1)],
                                                Qst[:, b % 2, h0 + h, P * j:S], start=True, stop=True)
                    last.then_inc(exp_filled, 1)
                at = attention_at(t, PV_START)
                if at and at[1] in PV_AT:
                    g, j = at[0], PV_AT.index(at[1])
                    b, h0 = g // GB, HG * (g % GB)
                    if j == 0:
                        pe.wait_ge(masked, 2 * (g + 1))
                        wait_drained(pe, "v", b)
                        if g:
                            pe.wait_ge(out_drained, g)
                    for h in range(HG):
                        bk, c0 = strip(h, j)
                        last = nc.tensor.matmul(ps_out[CW * h:CW * (h + 1), P * j:S], Vst[:, b % 2, j, h0 + h],
                                                Pr[:, g % 2, bk, c0:c0 + S - P * j], start=j == 0, stop=j == NT - 1)
                    if j == NT - 1:
                        last.then_inc(out_filled, 1)
            n, m = B - 1, len(NORMS) - 1
            pieces = [(c, t) for c in range(2) for t in range(B)]

            def gate_with_state(i):
                if i == 0:
                    pe.wait_ge(max_drained, NBANK * G)
                    pe.wait_ge(state_ready, B)
                for cols, _ in HALVES:
                    nc.tensor.matmul(ps_gate[i][:, cols], ffn_wT[:, 4 + i], state2[:, cols], start=cols.start == 0, stop=False,
                                     skip_group_check=True)

            def output_with_input(k):
                c, t = pieces[k]
                cols = HALVES[c][0]
                nc.tensor.matmul(ps_piece[k][:, cols], ffn_wT[:, 3], h2T[:, t, cols], start=True, stop=False)

            for c, (_, tiles) in enumerate(HALVES):
                take_shared(f"last_half{c}", n)
                pe.wait_ge(out_drained, G + c)
                for i in tiles:
                    last = nc.tensor.transpose(ps_half[c][:, P * i:P * (i + 1)], oT[:, (G - 1) % 2, P * i:P * (i + 1)], ident[:])
                last.then_inc(last_outT, 1)
            gate_with_state(0)
            for c, (_, tiles) in enumerate(HALVES):
                pe.wait_ge(attn_ready, B)
                pe.wait_ge(last_attn, c + 1)
                for i in tiles:
                    last = nc.tensor.transpose(ps_half[c][:, P * i:P * (i + 1)], attn[:, i], ident[:])
                last.then_inc(last_attnT, 1)
            gate_with_state(1)
            for c, (_, tiles) in enumerate(HALVES):
                pe.wait_ge(last_attnT_copied, c + 1)
                for i in tiles:
                    last = nc.tensor.matmul(ps_half[c][:, P * i:P * (i + 1)], attnT[:, P * i:P * (i + 1)], wo_gated[:, n], start=True, stop=True)
                last.then_inc(last_wo, 1)
            gate_with_state(2)
            pe.wait_ge(exp_drained, NBANK * G)
            for k in range(B - 1):
                output_with_input(k)
            for c, (_, tiles) in enumerate(HALVES):
                for i in tiles:
                    pe.wait_ge(ln_z, NT * m + i + 1)
                    last = nc.tensor.transpose(ps_half[c][:, P * i:P * (i + 1)], z_sb[:, m % 2, i], ident[:])
                last.then_inc(last_lnT, 1)
            for c, (cols, _) in enumerate(HALVES):
                pe.wait_ge(last_h2T, c + 1)
                for i in range(3):
                    last = nc.tensor.matmul(ps_gate[i][:, cols], ffn_wT[:, i], h2T[:, n, cols], start=False, stop=True,
                                            skip_group_check=True)
                    if c == 1:
                        last.then_inc(gate_filled, 1)
            output_with_input(B - 1)
            output_with_input(B)
            for i in range(3):
                pe.wait_ge(gate_ready, (1, 2, 4)[i])
                output_with_input(B + 1 + i)
            for k in range(len(pieces) + 2):
                if k < len(pieces):
                    c, t = pieces[k]
                    cols = HALVES[c][0]
                    if t == 0:
                        pe.wait_ge(state_ready, B + c + 1)
                    nc.tensor.matmul(ps_piece[k][:, cols], ffn_wT[:, 7], state2[:, cols], start=False, stop=True).then_inc(h_filled, 1)
                if k >= 2:
                    c, t = pieces[k - 2]
                    pe.wait_ge(hg_ready, k - 1)
                    for i in HALVES[c][1]:
                        last = nc.tensor.transpose(ps_piece[k - 2][:, P * i:P * (i + 1)], hg[:, t, P * i:P * (i + 1)], ident[:])
                    last.then_inc(y_filled, 1)


_INS = ["L0_attn_x", "L0_attn_WQ", "L0_attn_WK", "L0_attn_WV", "L0_attn_WO", "L0_ffn_wf", "L0_ffn_uf", "L0_ffn_bf",
        "L0_ffn_wi", "L0_ffn_ui", "L0_ffn_bi", "L0_ffn_wc", "L0_ffn_uc", "L0_ffn_bc", "L0_ffn_wo", "L0_ffn_uo",
        "L0_ffn_bo", "L0_ffn_in_c", "L0_c", "L0_wmod"]


def kernel(**inputs):
    import numpy as np
    import concourse.bacc as bacc
    from concourse.bass_utils import run_bass_kernel_spmd

    nc = bacc.Bacc("TRN2", target_bir_lowering=False, num_devices=1)
    arrays, args = {}, []
    for name in _INS:
        a = np.ascontiguousarray(inputs[name])
        arrays[f"in_{name}"] = a
        args.append(nc.dram_tensor(f"in_{name}", a.shape, mybir.dt.from_np(a.dtype), kind="ExternalInput").ap())
    out = nc.dram_tensor("out", (B, S, D), F32, kind="ExternalOutput").ap()
    adaln_block(nc, *args, out)
    r = run_bass_kernel_spmd(nc, [arrays], core_ids=[0])
    return r.results[0]["out"]
```
